# Optimizing a Trainium2 kernel written in Bass

```python
import numpy as np
import jax
import jax.numpy as jnp

def _softmax(x, axis=-1):
    return jax.nn.softmax(x, axis=axis)

def _gelu(x):
    return jax.nn.gelu(x, approximate=True)

def _silu(x):
    return jax.nn.silu(x)

def _sigmoid(x):
    return jax.nn.sigmoid(x)

def _layernorm(x, axis=-1, eps=1e-05):
    m = jnp.mean(x, axis=axis, keepdims=True)
    v = jnp.var(x, axis=axis, keepdims=True)
    return (x - m) / jnp.sqrt(v + eps)

def _scatter_add(tgt, idx, src, axis=0):
    return tgt.at[idx].add(src)

def _segment_sum(src, seg, n):
    return jax.ops.segment_sum(src, seg, n)
kernel_name = 'mk_cond_resid_d2_seqx_r8_51d876'

def setup_inputs(seed: int=0):
    np.random.seed(seed)
    _w = jnp.asarray

    def _rec_inputs():
        import jax
        import jax.numpy as jnp
        _rk = jax.random.key(seed)
        x = 7.22e-05 + 1 * jax.random.normal(jax.random.fold_in(_rk, 1), (8, 128, 256), jnp.float32)
        _lenS = 128 - jax.random.randint(jax.random.fold_in(_rk, 7), (8,), 0, max(1, 128 // 4) + 1, jnp.int32)
        _lenS2 = 128 - jax.random.randint(jax.random.fold_in(_rk, 8), (8,), 0, max(1, 128 // 4) + 1, jnp.int32)
        cond_2048 = jax.random.bernoulli(jax.random.fold_in(_rk, 11), 0.5063, (8, 256)).astype(jnp.float32)
        return (x, cond_2048)
    x, cond_2048 = _rec_inputs()

    def _L0_cond_setup():
        import jax, jax.numpy as jnp
        import numpy as np
        NH = 8
        NEG = -1e+30
        key = jax.random.key(seed)
        k1, k2, k3, k4 = jax.random.split(key, 4)
        B, D, T = (4, 128, 256)
        x = jax.random.normal(k1, (B, D, T), dtype=jnp.float32)
        mask = jax.random.randint(k2, (B, T), 0, 2).astype(jnp.float32)
        lim = float(np.sqrt(6.0 / (D + D)))
        Wq = jax.random.uniform(k3, (D, D), dtype=jnp.float32, minval=-lim, maxval=lim)
        Wo = jax.random.uniform(k4, (D, D), dtype=jnp.float32, minval=-lim, maxval=lim)
        return {'x': x, 'mask': mask, 'Wq': Wq, 'Wo': Wo}
    _L0_cond_all = _L0_cond_setup()
    _L0_cond_in = {k: v for k, v in _L0_cond_all.items() if k in ('Wq', 'Wo')}
    del _L0_cond_all

    def _L1_cond_setup():
        import jax, jax.numpy as jnp
        import numpy as np
        DIM = 256
        H = 16
        DH = 128
        INNER = H * DH
        MLP = 4 * DIM
        B, T = (2, 256)
        EPS = 1e-06

        def _ln(x):
            mu = jnp.mean(x, axis=-1, keepdims=True)
            var = jnp.var(x, axis=-1, keepdims=True)
            return (x - mu) * jax.lax.rsqrt(var + EPS)
        key = jax.random.key(seed)
        ks = jax.random.split(key, 12)
        s = 0.02
        return {'x': jax.random.normal(ks[0], (B, T, DIM), jnp.float32), 'timestep_embed': jax.random.normal(ks[1], (B, DIM), jnp.float32), 'ada_w': jax.random.normal(ks[2], (DIM, 6 * DIM), jnp.float32) * s, 'ada_b': jnp.zeros((6 * DIM,), jnp.float32), 'qkv_w': jax.random.normal(ks[3], (DIM, 3 * INNER), jnp.float32) * s, 'qkv_b': jnp.zeros((3 * INNER,), jnp.float32), 'out_w': jax.random.normal(ks[4], (INNER, DIM), jnp.float32) * s, 'out_b': jnp.zeros((DIM,), jnp.float32), 'ffn_w1': jax.random.normal(ks[5], (DIM, MLP), jnp.float32) * s, 'ffn_b1': jnp.zeros((MLP,), jnp.float32), 'ffn_w2': jax.random.normal(ks[6], (MLP, DIM), jnp.float32) * s, 'ffn_b2': jnp.zeros((DIM,), jnp.float32)}
    _L1_cond_all = _L1_cond_setup()
    _L1_cond_in = {k: v for k, v in _L1_cond_all.items() if k in ('ada_w', 'ada_b', 'qkv_w', 'qkv_b', 'out_w', 'out_b', 'ffn_w1', 'ffn_b1', 'ffn_w2', 'ffn_b2')}
    del _L1_cond_all
    return {'x': x, 'cond_2048': cond_2048, 'L0_cond_Wq': _L0_cond_in['Wq'], 'L0_cond_Wo': _L0_cond_in['Wo'], 'L1_cond_ada_w': _L1_cond_in['ada_w'], 'L1_cond_ada_b': _L1_cond_in['ada_b'], 'L1_cond_qkv_w': _L1_cond_in['qkv_w'], 'L1_cond_qkv_b': _L1_cond_in['qkv_b'], 'L1_cond_out_w': _L1_cond_in['out_w'], 'L1_cond_out_b': _L1_cond_in['out_b'], 'L1_cond_ffn_w1': _L1_cond_in['ffn_w1'], 'L1_cond_ffn_b1': _L1_cond_in['ffn_b1'], 'L1_cond_ffn_w2': _L1_cond_in['ffn_w2'], 'L1_cond_ffn_b2': _L1_cond_in['ffn_b2']}

def reference(x, cond_2048, L0_cond_Wq, L0_cond_Wo, L1_cond_ada_w, L1_cond_ada_b, L1_cond_qkv_w, L1_cond_qkv_b, L1_cond_out_w, L1_cond_out_b, L1_cond_ffn_w1, L1_cond_ffn_b1, L1_cond_ffn_w2, L1_cond_ffn_b2):
    import jax
    import jax.numpy as jnp

    def _L0_cond_ref(x, mask, Wq, Wo):
        import jax, jax.numpy as jnp
        import numpy as np
        NH = 8
        NEG = -1e+30
        B, D, T = x.shape
        dk = D // NH
        scale = 1.0 / jnp.sqrt(jnp.asarray(dk, x.dtype))
        xt = jnp.transpose(x, (0, 2, 1))
        q = xt @ Wq.T
        qh = q.reshape(B, T, NH, dk).transpose(0, 2, 1, 3)
        scores = scale * jnp.einsum('bhqd,bhkd->bhqk', qh, qh)
        cmask = mask[:, None, None, :]
        rmask = mask[:, None, :, None]
        logits = (scores * cmask + (1.0 - cmask) * NEG) * rmask
        attn = jax.nn.softmax(logits, axis=-1)
        ctx = jnp.einsum('bhqk,bhkd->bhqd', attn, qh)
        ctx = ctx.transpose(0, 2, 1, 3).reshape(B, T, D)
        out = ctx @ Wo.T
        return jnp.transpose(out, (0, 2, 1))

    def _L1_cond_ref(x, timestep_embed, ada_w, ada_b, qkv_w, qkv_b, out_w, out_b, ffn_w1, ffn_b1, ffn_w2, ffn_b2):
        import jax, jax.numpy as jnp
        import numpy as np
        DIM = 256
        H = 16
        DH = 128
        INNER = H * DH
        MLP = 4 * DIM
        B, T = (2, 256)
        EPS = 1e-06

        def _ln(x):
            mu = jnp.mean(x, axis=-1, keepdims=True)
            var = jnp.var(x, axis=-1, keepdims=True)
            return (x - mu) * jax.lax.rsqrt(var + EPS)
        Bc, Tc, D = x.shape
        ada = (timestep_embed @ ada_w + ada_b)[:, None, :]
        shift1, scale1, gate1, shift2, scale2, gate2 = jnp.split(ada, 6, axis=-1)
        x1 = _ln(x) * (1.0 + scale1) + shift1
        qkv = (x1 @ qkv_w + qkv_b).reshape(Bc, Tc, 3, H, DH)
        q, k, v = (qkv[:, :, 0], qkv[:, :, 1], qkv[:, :, 2])
        scale = DH ** (-0.5)
        attn = jnp.einsum('bthd,bshd->bhts', q, k) * scale
        attn = jax.nn.softmax(attn, axis=-1)
        attn_out = jnp.einsum('bhts,bshd->bthd', attn, v).reshape(Bc, Tc, INNER)
        attn_out = attn_out @ out_w + out_b
        x = x + gate1 * attn_out
        x2 = _ln(x) * (1.0 + scale2) + shift2
        h = jax.nn.gelu(x2 @ ffn_w1 + ffn_b1, approximate=False)
        x = x + gate2 * (h @ ffn_w2 + ffn_b2)
        return x
    x = x + _L0_cond_ref(x, cond_2048, L0_cond_Wq, L0_cond_Wo)
    x = x + _L1_cond_ref(x, cond_2048, L1_cond_ada_w, L1_cond_ada_b, L1_cond_qkv_w, L1_cond_qkv_b, L1_cond_out_w, L1_cond_out_b, L1_cond_ffn_w1, L1_cond_ffn_b1, L1_cond_ffn_w2, L1_cond_ffn_b2)
    return x

_drawn_inputs = setup_inputs


def setup_inputs(seed=0):
    import zlib

    import numpy as np

    out = dict(_drawn_inputs(seed))
    spreads = {'L1_cond_ada_b': (0.0, 0.763),
     'L1_cond_qkv_b': (0.0, 0.702),
     'L1_cond_out_b': (0.0, 0.716),
     'L1_cond_ffn_b1': (0.0, 0.8),
     'L1_cond_ffn_b2': (0.0, 0.683)}
    factors = {'L1_cond_qkv_w': 5.857,
     'L1_cond_out_w': 3.788,
     'L1_cond_ffn_w1': 4.244,
     'L1_cond_ffn_w2': 3.897}
    for name, (base, spread) in spreads.items():
        noise = np.random.default_rng([zlib.crc32(name.encode()), seed]).standard_normal(out[name].shape)
        drawn = base * np.exp(spread * noise) if base else spread * noise
        out[name] = jnp.asarray(drawn.astype(out[name].dtype))
    for name, factor in factors.items():
        out[name] = (out[name] * factor).astype(out[name].dtype)
    return out
```

```python
from contextlib import ExitStack

import concourse.bass as bass
from concourse import mybir

F32 = mybir.dt.float32
F32R = mybir.dt.float32r
ALU = mybir.AluOpType
ACT = mybir.ActivationFunctionType
AX = mybir.AxisListType

P = 128
B = 8
T = 256
D = 128
NH0, DK = 8, 16
NH1, DH = 16, 128
DIM, INNER, MLP = T, NH1 * DH, 4 * T
KT = DIM // P
NEG = 1e30
LN_EPS = 1e-6
SCALE1 = float(DH) ** -0.5

HEAD_ROWS = 64
MASK_ROW = 3 * DK
MAX_ROW = MASK_ROW + 3
PAIRS = NH0 // 2
HPG = 4
GROUPS = NH1 // HPG
CH = B // 2
CT = CH * D
STEPS = GROUPS * 2 * HPG
MB = MLP // P


def row_roles():
    import numpy as np
    t = np.zeros((P, 5), np.float32)
    t[1, 4] = -1.0
    for i in range(2):
        o = i * HEAD_ROWS
        t[o:o + 3 * DK, 2] = 0.25
        t[o + DK:o + 2 * DK, 1] = -1.0
        t[o + 2 * DK:o + 3 * DK, 0] = -1.0
        t[o + MASK_ROW:o + MASK_ROW + 3, 2] = NEG
        t[o + MASK_ROW:o + MASK_ROW + 3, 3] = -NEG
        t[o + MASK_ROW + 1, 1] = -1.0
        t[o + MASK_ROW + 2, 0] = -1.0
        t[o + MAX_ROW:o + MAX_ROW + 2, 3] = 1.0
    return t


def build_program(nc, x, cond, cond_t, wq_t, wo_t, ada_w, ada_b, ada_b_t, qkv_w, qkv_b_t, out_w, out_b,
                  ffn_w1, ffn_b1_t, ffn_w2, ffn_b2, roles, out):
    ctx = ExitStack()
    with ctx:
        def sb(name, shape, dt=F32):
            return ctx.enter_context(nc.sbuf_tensor(name, shape, dt))

        def sem(name):
            return ctx.enter_context(nc.semaphore(name))

        ident = sb("ident", [P, P])
        role = sb("role", [P, 5])
        temb_t = sb("temb_t", [P, KT, B])
        ada_bt = sb("ada_bt", [P, 12])
        gate_b = sb("gate_b", [B, 2, DIM])
        qkv_bt = sb("qkv_bt", [P, 3 * NH1])
        q_bias = sb("q_bias", [P, NH1])
        b1_t = sb("b1_t", [P, MB])
        out_b_bc = sb("out_b_bc", [P, DIM])
        b2_bc = sb("b2_bc", [P, DIM])
        mod = sb("mod", [P, 8, B])
        gates = sb("gates", [B, 2, DIM])
        sel = sb("sel", [B, B, P])
        pw = sb("pw", [P, B])
        stats = sb("stats", [P, B, 6])
        mv = sb("mv", [P, B, 2])
        veps = sb("veps", [P, B])
        rstd = sb("rstd", [P, B])
        xm = sb("xm", [P, B, DIM])
        acc = sb("acc", [P, B, DIM])
        xh = sb("xh", [P, KT, B * D], F32R)
        xl = sb("xl", [P, KT, B * D], F32R)
        w_raw = [sb(f"w_raw{i}", [P, KT, 3, HPG * DH]) for i in range(2)]
        w_qk_h = sb("w_qk_h", [P, KT, 2, HPG * DH], F32R)
        w_qk_l = sb("w_qk_l", [P, KT, 2, HPG * DH], F32R)
        w_v_h = sb("w_v_h", [P, 2, KT, HPG * DH], F32R)
        w_v_l = sb("w_v_l", [P, 2, KT, HPG * DH], F32R)

        banks = [ctx.enter_context(nc.psum_tensor(f"bank{i}", [P, 512], F32)) for i in range(8)]
        s_xin = [sem(f"s_xin{b}") for b in range(B)]
        s_ld = {k: sem("s_ld_" + k) for k in ("small0", "cond", "wq", "wo", "small1", "ada")}
        s_wraw = [sem(f"s_wraw{i}") for i in range(2)]
        S = {}

        def s(name):
            if name not in S:
                S[name] = sem("s_" + name)
            return S[name]

        l0 = ExitStack()

        def sb0(name, shape, dt=F32):
            return l0.enter_context(nc.sbuf_tensor(name, shape, dt))

        x_in = sb0("x_in", [P, B, T])
        rbc = sb0("rbc", [P, B, T])
        c_rows = acc[0:2, :, :].rearrange("p b t -> p (b t)")
        c_hi = xh[0:2, :, :].rearrange("p k t -> p (k t)")
        r_rows = sb0("r_rows", [2, B, T], F32R)
        e_rows = sb0("e_rows", [2, P], F32R)
        w_q = sb0("w_q", [P, P])
        w_rep = sb0("w_rep", [P, PAIRS, P])
        w_o = sb0("w_o", [P, P])
        ones_c = sb0("ones_c", [P, 2, 32])
        xr = [sb0(f"xr{i}", [P, T]) for i in range(2)]
        zh = sb0("zh", [P, PAIRS, T], F32R)
        zr = sb0("zr", [P, PAIRS, T])
        zrh = sb0("zrh", [P, PAIRS, T], F32R)
        left = [sb0(f"left{i}", [P, PAIRS, T], F32R) for i in range(2)]
        leftm = [sb0(f"leftm{i}", [P, PAIRS, T], F32R) for i in range(2)]
        right = [sb0(f"right{i}", [P, PAIRS, T], F32R) for i in range(3)]
        nmax = sb0("nmax", [P, NH0, 2])
        nmax_h = sb0("nmax_h", [P, NH0, 2], F32R)
        mx = sb0("mx", [P, 2, 2, 2, P])
        pt = sb0("pt", [P, NH0, 2, T])
        vp = [sb0(f"vp{i}", [P, 2, NH0, 32]) for i in range(2)]
        dinv = sb0("dinv", [P, T])
        cn = sb0("cn", [P, T])

        bank_z = banks[0:2]
        bank_a, bank_s = banks[2:4], banks[4:6]
        bank_c, bank_m = banks[6], banks[7]

        blk = l0.enter_context(nc.Block())

        @blk.sync
        def _(sp):
            sp.dma_start(w_q[:, :], wq_t).then_inc(s_ld["wq"], 16)
            sp.dma_start(c_rows, cond.rearrange("b t -> (b t)").partition_broadcast(2)).then_inc(s_ld["cond"], 16)
            for b in range(B):
                sp.dma_start(x_in[:, b, :], x[b]).then_inc(s_xin[b], 16)
                if b == 0:
                    sp.dma_start(rbc[:, :, :], cond.partition_broadcast(P)).then_inc(s_ld["cond"], 16)
                    sp.dma_start(role[:, :], roles).then_inc(s_ld["small0"], 16)
            for h in range(NH0):
                r = 32 * (h % 4) + 16 * (h // 4)
                sp.dma_start(w_o[r:r + DK, :], wo_t[h * DK:(h + 1) * DK, :]).then_inc(s_ld["wo"], 16)
            sp.dma_start(temb_t[:, :, :], cond_t.rearrange("(k p) b -> p k b", p=P)).then_inc(s_ld["small1"], 16)
            sp.dma_start(ada_bt[:, :], ada_b_t).then_inc(s_ld["small1"], 16)
            for g in range(2):
                sp.dma_start(gate_b[:, g, :], ada_b[(3 * g + 2) * DIM:(3 * g + 3) * DIM].partition_broadcast(B))\
                  .then_inc(s_ld["small1"], 16)
            sp.dma_start(qkv_bt[:, :], qkv_b_t).then_inc(s_ld["small1"], 16)
            sp.dma_start(b1_t[:, :], ffn_b1_t).then_inc(s_ld["small1"], 16)
            sp.dma_start(out_b_bc[:, :], out_b.partition_broadcast(P)).then_inc(s_ld["small1"], 16)
            sp.dma_start(b2_bc[:, :], ffn_b2.partition_broadcast(P)).then_inc(s_ld["small1"], 16)
            for k in range(KT):
                sp.dma_start(w_raw[1][:, k, :, :].rearrange("p s n -> p (s n)"), ada_w[k * P:(k + 1) * P, :])\
                  .then_inc(s_ld["ada"], 16)
            for k in range(KT):
                sp.dma_start(w_raw[0][:, k, :, :],
                             qkv_w[k * P:(k + 1) * P, :].rearrange("p (s n) -> p s n", s=3)[:, :, 0:HPG * DH])\
                  .then_inc(s_wraw[0], 16)

        @blk.gpsimd
        def _(pool):
            pool.memset(w_rep[:, :, :], 0.0).then_inc(s("memset"), 1)
            pool.memset(e_rows[:, :].bitcast(F32), 0.0).then_inc(s("memset"), 1)
            pool.memset(ident[:, :], 0.0).then_inc(s("memset"), 1)
            pool.memset(mx[:, :, :, :, :], 0.0).then_inc(s("mx0"), 1)
            pool.memset(ones_c[:, :, :], 0.0).then_inc(s("memset"), 1)
            for i in range(2):
                pool.memset(vp[i][:, :, :, :], 0.0).then_inc(s("vp0"), 1)
            pool.memset(sel[:, :, :], 0.0).then_inc(s("memset"), 1)
            pool.memset(pw[:, :], -0.5).then_inc(s("pw"), 1)
            pool.wait_ge(s("memset"), 5)
            pool.memset(e_rows[:, :].bitcast(F32).rearrange("p (i r) -> p i r", i=2)[:, :, MASK_ROW:MASK_ROW + 3], 1.0)\
                .then_inc(s("const"), 1)
            for a in range(2):
                pool.memset(ones_c[:, a, 16 * a:16 * a + 16], 1.0).then_inc(s("const"), 1)
            pool.affine_select(out=ident[:, :], in_=ident[:, :], compare_op=ALU.not_equal, fill=1.0, base=0,
                               pattern=[[-1, P]], channel_multiplier=1).then_inc(s("const"), 1)
            pool.affine_select(out=sel[:, :, :], in_=sel[:, :, :], compare_op=ALU.not_equal, fill=1.0, base=0,
                               pattern=[[-1, B], [0, P]], channel_multiplier=1).then_inc(s("const"), 1)
            pool.wait_ge(s_ld["wq"], 16)
            for k in range(3):
                pool.tensor_copy(w_rep[:, :, :].rearrange("p g (i r) -> p (g i) r", i=2)[:, :, k * DK:(k + 1) * DK],
                                 w_q[:, :].rearrange("p (h e) -> p h e", e=DK)).then_inc(s("wrep"), 1)

            def masked_x(b):
                pool.wait_ge(s_xin[b], 16)
                if b == 0:
                    pool.wait_ge(s_ld["cond"], 32)
                if b >= 2:
                    pool.wait_ge(s("z"), 2 * (b - 1))
                pool.tensor_tensor(xr[b % 2][:, :], x_in[:, b, :], rbc[:, b, :], ALU.mult).then_inc(s("xr"), 1)

            masked_x(0)
            masked_x(1)
            for b in range(B):
                if b + 2 < B:
                    masked_x(b + 2)

        @blk.tensor
        def _(pe):
            def queries(b, n):
                pe.wait_ge(s("xr"), b + 1)
                if b >= 1:
                    pe.wait_ge(s("left"), 2 * b - 1 + n)
                pe.matmul(bank_z[n][:, :], e_rows[:, :],
                          r_rows[:, b, :].unsqueeze(1).to_broadcast([2, 2, T]), start=True, stop=False)
                for i in range(2):
                    mm = pe.matmul(bank_z[n][:, i * T:(i + 1) * T], w_rep[:, 2 * n + i, :], xr[b % 2][:, :],
                                   start=False, stop=(i == 1))
                mm.then_inc(s("z"), 1)

            def values(b):
                pe.wait_ge(s_xin[b], 16)
                if b >= 1:
                    pe.wait_ge(s("leftm"), 2 * b)
                for k in range(2):
                    mm = pe.matmul(bank_m[:, k * P:(k + 1) * P], x_in[:, b, k * P:(k + 1) * P], w_q[:, :],
                                   start=True, stop=True)
                mm.then_inc(s("v"), 1)

            def scores_qk(b, h):
                n = b * NH0 + h
                if n >= 2:
                    pe.wait_ge(s("max"), n - 1)
                g, o = h // 2, HEAD_ROWS * (h % 2)
                for k in range(2):
                    mm = pe.matmul(bank_a[n % 2][:, k * T:(k + 1) * T],
                                   left[b % 2][o:o + MAX_ROW, g, k * P:(k + 1) * P],
                                   right[b % 3][o:o + MAX_ROW, g, :], start=True, stop=True)
                mm.then_inc(s("a"), 1)

            def scores_kq(b, h):
                n = b * NH0 + h
                if n >= 2:
                    pe.wait_ge(s("exp"), n - 1)
                g, o = h // 2, HEAD_ROWS * (h % 2)
                for k in range(2):
                    mm = pe.matmul(bank_s[n % 2][:, k * T:(k + 1) * T],
                                   right[b % 3][o:o + MAX_ROW + 2, g, k * P:(k + 1) * P],
                                   leftm[b % 2][o:o + MAX_ROW + 2, g, :], start=True, stop=True)
                mm.then_inc(s("s"), 1)

            def max_rows(b, half):
                n = 2 * b + half
                pe.wait_ge(s("mx"), n + 1)
                if half == 0:
                    pe.wait_ge(s("vp"), b + 1)
                    if b >= 2:
                        pe.wait_ge(s("xm"), b - 1)
                else:
                    pe.wait_ge(s("leftm"), n)
                for g in range(2):
                    for k in range(2):
                        mm = pe.transpose(bank_m[:, (2 * g + k) * P:(2 * g + k + 1) * P],
                                          mx[:, half, k, g, :], ident[:, :])
                mm.then_inc(s("t"), 1)

            def weigh(b, a, k):
                pe.wait_ge(s("exp"), b * NH0 + 4 * a + 4)
                if a == 0 and k == 0:
                    pe.wait_ge(s("vp"), b + 1)
                    if b >= 1:
                        pe.wait_ge(s("cn"), b)
                for what in range(2):
                    for j in range(4):
                        h = 4 * a + j
                        lhs = ones_c[:, a, :] if what else vp[b % 2][:, k, h, :]
                        mm = pe.matmul(bank_c[32 * j:32 * j + 32, what * T:(what + 1) * T], lhs,
                                       pt[:, h, k, :], start=(a == 0 and k == 0 and what == 0),
                                       stop=(a == 1 and k == 1), skip_group_check=True)
                mm.then_inc(s("c"), 1)

            def project(b):
                pe.wait_ge(s("cn"), b + 1)
                if b == 0:
                    pe.wait_ge(s_ld["wo"], 16 * NH0)
                pe.wait_ge(s("vp"), min(b + 3, B))
                if b == B - 1:
                    pe.wait_ge(s("leftm"), 2 * B)
                pe.matmul(bank_m[:, 0:T], w_o[:, :], cn[:, :], start=True, stop=True).then_inc(s("o"), 1)

            pe.wait_ge(s_ld["wq"], 16)
            pe.wait_ge(s("const"), 5)
            pe.wait_ge(s("wrep"), 3)
            pe.wait_ge(s("rrows"), 1)
            queries(0, 0)
            queries(0, 1)
            for b in range(-1, B + 1):
                for h in range(NH0):
                    if 0 <= b < B:
                        if h == 0:
                            pe.wait_ge(s("leftm"), 2 * b + 1)
                        if h == 4:
                            pe.wait_ge(s("leftm"), 2 * b + 2)
                        scores_kq(b, h)
                    if b + 1 < B:
                        if h == 0:
                            pe.wait_ge(s("left"), 2 * (b + 2))
                            pe.wait_ge(s("right"), 2 * (b + 2))
                        scores_qk(b + 1, h)
                    if h == 0 and b >= 1:
                        weigh(b - 1, 1, 0)
                    if h == 1 and 0 <= b < B:
                        max_rows(b, 1)
                    if h == 1 and b >= 1:
                        weigh(b - 1, 1, 1)
                    if h in (2, 3) and b + 2 < B:
                        queries(b + 2, h - 2)
                    if h == 2 and b + 1 < B:
                        values(b + 1)
                    if h == 4 and b >= 1:
                        project(b - 1)
                    if h == 5 and b + 1 < B:
                        max_rows(b + 1, 0)
                    if h in (5, 6) and 0 <= b < B:
                        weigh(b, 0, h - 5)

        @blk.scalar
        def _(act):
            act.wait_ge(s_ld["cond"], 32)
            act.activation(c_hi, c_rows, ACT.Copy).then_inc(s("rhi"), 1)
            act.wait_ge(s_ld["small0"], 16)

            def stack(b, n):
                act.wait_ge(s("z"), 2 * b + n + 1)
                if b >= 1:
                    act.wait_ge(s("right"), 2 * b - 1 + n)
                    act.wait_ge(s("left"), 2 * b - 1 + n)
                two = slice(2 * n, 2 * n + 2)
                act.activation(zr[:, two, :].rearrange("p g t -> p (g t)"), bank_z[n][:, :], ACT.Identity,
                               bias=role[:, 3:4], scale=role[:, 2:3])
                act.activation(zrh[:, two, :].rearrange("p g t -> p (g t)"), bank_z[n][:, :], ACT.Identity,
                               bias=role[:, 3:4], scale=role[:, 2:3]).then_inc(s("zr"), 1)
                act.activation(zh[:, two, :].rearrange("p g t -> p (g t)"), bank_z[n][:, :], ACT.Copy)\
                   .then_inc(s("zh"), 1)

            def value_cols(b):
                act.wait_ge(s("v"), b + 1)
                if b == 0:
                    act.wait_ge(s("vp0"), 2)
                if b >= 2:
                    act.wait_ge(s("c"), 4 * (b - 1))
                v = bank_m[:, 0:2 * P].rearrange("p (k a je) -> p k a je", k=2, a=2)
                for a in range(2):
                    for k in range(2):
                        last = act.activation(vp[b % 2][:, k, 4 * a:4 * a + 4, 16 * a:16 * a + 16],
                                              v[:, k, a, :].rearrange("p (j e) -> p j e", e=DK), ACT.Copy)
                last.then_inc(s("vp"), 1)

            stack(0, 0)
            stack(0, 1)
            for b in range(-1, B):
                for h in range(NH0):
                    if b >= 0:
                        n = b * NH0 + h
                        act.wait_ge(s("s"), n + 1)
                        if b >= 1 and h % 4 == 0:
                            act.wait_ge(s("c"), 4 * (b - 1) + 2 * (h // 4 + 1))
                        act.activation(pt[:, h, :, :].rearrange("p k t -> p (k t)"), bank_s[n % 2][:, :], ACT.Exp)\
                           .then_inc(s("exp"), 1)
                    if h in (2, 3) and b + 2 < B:
                        stack(b + 2, h - 2)
                    if h == 2 and b + 1 < B:
                        value_cols(b + 1)

        @blk.vector
        def _(dve):
            dve.wait_ge(s("rhi"), 1)
            dve.wait_ge(s_ld["small0"], 16)
            dve.scalar_tensor_tensor(out=r_rows[:, :, :].rearrange("p b t -> p (b t)"), in0=c_hi.bitcast(F32),
                                     scalar=role[0:2, 4:5], in1=c_rows, op0=ALU.mult, op1=ALU.add)\
               .then_inc(s("rrows"), 1)

            def left_op(b, n):
                dve.wait_ge(s("zh"), 2 * b + n + 1)
                if b >= 2:
                    dve.wait_ge(s("a"), (b - 1) * NH0)
                    dve.wait_ge(s("leftm"), 2 * (b - 1))
                two = slice(2 * n, 2 * n + 2)
                dve.scalar_tensor_tensor(
                    out=left[b % 2][:, two, :].rearrange("p g t -> p (g t)"),
                    in0=zh[:, two, :].rearrange("p g t -> p (g t)").bitcast(F32), scalar=role[:, 0:1],
                    in1=bank_z[n][:, :], op0=ALU.mult, op1=ALU.add).then_inc(s("left"), 1)

            def right_op(b, n):
                dve.wait_ge(s("zr"), 2 * b + n + 1)
                if b >= 3:
                    dve.wait_ge(s("s"), (b - 2) * NH0)
                two = slice(2 * n, 2 * n + 2)
                dve.scalar_tensor_tensor(out=right[b % 3][:, two, :], in0=zrh[:, two, :].bitcast(F32),
                                         scalar=role[:, 1:2], in1=zr[:, two, :], op0=ALU.mult, op1=ALU.add)\
                   .then_inc(s("right"), 1)

            def max_split(b, half):
                n = 2 * b + half
                dve.wait_ge(s("max"), b * NH0 + 4 * half + 4)
                src = nmax[:, 4 * half:4 * half + 4, :]
                hi = nmax_h[:, 4 * half:4 * half + 4, :]
                dve.tensor_copy(hi, src).then_inc(s("nh"), 1)
                dve.wait_ge(s("nh"), n + 1)
                if n == 0:
                    dve.wait_ge(s("mx0"), 1)
                if n >= 2:
                    dve.wait_ge(s("t"), n - 1)
                dst = mx[:, half, :, :, :].rearrange("p k g (i r) -> p g i k r", i=2)
                s4 = src.rearrange("p (g i) k -> p g i k", i=2)
                h4 = hi.rearrange("p (g i) k -> p g i k", i=2).bitcast(F32)
                dve.tensor_copy(dst[:, :, :, :, MAX_ROW], h4)
                dve.tensor_tensor(dst[:, :, :, :, MAX_ROW + 1], s4, h4, ALU.subtract).then_inc(s("mx"), 1)

            def left_with_max(b, half):
                n = 2 * b + half
                dve.wait_ge(s("t"), n + 1)
                if b >= 2:
                    dve.wait_ge(s("s"), (b - 1) * NH0)
                dve.wait_ge(s("left"), 2 * b + 1 + half)
                dve.tensor_tensor(leftm[b % 2][:, 2 * half:2 * half + 2, :].rearrange("p g t -> p (g t)"),
                                  bank_m[:, :],
                                  left[b % 2][:, 2 * half:2 * half + 2, :].rearrange("p g t -> p (g t)").bitcast(F32),
                                  ALU.add).then_inc(s("leftm"), 1)

            def inverse_sums(b, i):
                if i == 0:
                    dve.wait_ge(s("c"), 4 * b + 4)
                dve.reciprocal(dinv[:, i * P:(i + 1) * P], bank_c[:, T + i * P:T + (i + 1) * P]).then_inc(s("dinv"), 1)

            def normalise(b):
                dve.wait_ge(s("dinv"), 2 * b + 2)
                if b >= 1:
                    dve.wait_ge(s("o"), b)
                dve.tensor_tensor(cn[:, :], bank_c[:, 0:T], dinv[:, :], ALU.mult).then_inc(s("cn"), 1)

            for n in range(2):
                left_op(0, n)
            for n in range(2):
                right_op(0, n)
            for b in range(-1, B + 1):
                for h in range(NH0):
                    if b + 1 < B:
                        n = (b + 1) * NH0 + h
                        dve.wait_ge(s("a"), n + 1)
                        if h % 4 == 0 and n >= 8:
                            dve.wait_ge(s("mx"), 2 * b + h // 4 + 1)
                        dve.tensor_reduce(nmax[:, h, :], bank_a[n % 2][:, :].rearrange("p (k t) -> p k t", k=2),
                                          AX.X, ALU.max, negate=True).then_inc(s("max"), 1)
                        if h == 3:
                            max_split(b + 1, 0)
                        if h == 7:
                            max_split(b + 1, 1)
                    if h == 1 and 0 <= b < B:
                        left_with_max(b, 1)
                    if h in (2, 3) and b >= 1:
                        inverse_sums(b - 1, h - 2)
                    if h == 3 and b >= 1:
                        normalise(b - 1)
                    if h == 4 and b + 2 < B:
                        left_op(b + 2, 0)
                    if h == 4 and b >= 1:
                        dve.wait_ge(s("o"), b)
                        dve.tensor_tensor(xm[:, b - 1, :], bank_m[:, 0:T], x_in[:, b - 1, :], ALU.add)\
                           .then_inc(s("xm"), 1)
                    if h == 5 and b + 1 < B:
                        left_with_max(b + 1, 0)
                    if h == 6 and b + 2 < B:
                        left_op(b + 2, 1)
                        right_op(b + 2, 0)
                    if h == 7 and b + 2 < B:
                        right_op(b + 2, 1)

        l0.close()

        ow_raw = [sb(f"ow_raw{i}", [P, HPG, DIM]) for i in range(2)]
        ow_h = sb("ow_h", [P, NH1, DIM], F32R)
        ow_l = sb("ow_l", [P, NH1, DIM], F32R)
        v_sb = sb("v_sb", [P, 2, CH, HPG * DH])
        qk = sb("qk", [P, 2, 2, CT])
        prob = sb("prob", [P, 2, CH, D])
        prob_t = sb("prob_t", [P, 2, CH, D])
        at_h = sb("at_h", [P, 2, HPG, CT], F32R)
        at_l = sb("at_l", [P, 2, HPG, CT], F32R)
        xn = sb("xn", [P, 2, DIM])
        xn_f = sb("xn_f", [P, 2, KT, D])
        nm1 = sb("nm1", [P, 2, CH])
        sum1 = sb("sum1", [P, 2, CH])
        rs1 = sb("rs1", [P, 2, CH])

        ctx2 = ExitStack()
        blk = ctx2.enter_context(nc.Block())
        bank_p = banks[0:2]
        bank_s1 = banks[2:4]
        bank_t1, bank_v1, bank_o1, bank_g = banks[4], banks[5], banks[6], banks[7]
        HGROUPS = 2 * GROUPS

        w1_raw = w_raw[0][:, :, :, :].rearrange("p k s n -> p (k s n)")[:, 0:KT * MLP]\
            .rearrange("p (k n) -> p k n", k=KT)
        w2_raw = w_raw[1][:, :, :, :].rearrange("p k s n -> p (k s n)")[:, 0:MB * DIM]\
            .rearrange("p (m n) -> p m n", m=MB)
        w1_h = w_qk_h[:, :, :, :].rearrange("p k s n -> p k (s n)")
        w1_l = w_qk_l[:, :, :, :].rearrange("p k s n -> p k (s n)")
        w2_h = w_v_h[:, :, :, :].rearrange("p a k n -> p (a k n)").rearrange("p (m n) -> p m n", m=MB)
        w2_l = w_v_l[:, :, :, :].rearrange("p a k n -> p (a k n)").rearrange("p (m n) -> p m n", m=MB)

        h_h = at_h[:, :, :, :].rearrange("p a j n -> p (a j) n")
        h_l = at_l[:, :, :, :].rearrange("p a j n -> p (a j) n")
        h_f = v_sb[:, :, :, :].rearrange("p a j n -> p (a j) n")

        def part(n):
            m, k = divmod(n, HPG)
            return m, k, m // 2, m % 2

        proj_no = {}
        order = [("v", 0, k) for k in range(CH)] + [("q", 0), ("k", 0)]
        for n in range(STEPS):
            m, k, hg, c = part(n)
            if n + 1 < STEPS:
                order += [("q", n + 1), ("k", n + 1)]
            if m + 1 < HGROUPS:
                order += [("v", m + 1, k)]
        for i, what in enumerate(order):
            proj_no[what] = i

        @blk.sync
        def _(sp):
            def load_ow(g):
                if g >= 2:
                    sp.wait_ge(s("ow"), g - 1)
                sp.dma_start(ow_raw[g % 2][:, :, :],
                             out_w.rearrange("(h p) n -> p h n", p=P)[:, g * HPG:(g + 1) * HPG, :])\
                  .then_inc(s(f"ld_ow{g % 2}"), 16)

            load_ow(0)
            load_ow(1)
            sp.wait_ge(s("mod"), 1)
            for g in range(1, GROUPS):
                if g >= 2:
                    load_ow(g)
                    sp.wait_ge(s("wsplit"), 5 * (g - 1))
                for k in range(KT):
                    sp.dma_start(w_raw[g % 2][:, k, :, :],
                                 qkv_w[k * P:(k + 1) * P, :].rearrange("p (s n) -> p s n", s=3)
                                 [:, :, g * HPG * DH:(g + 1) * HPG * DH]).then_inc(s_wraw[g % 2], 16)
            sp.wait_ge(s("wsplit"), 5 * GROUPS)
            sp.dma_start(w1_raw, ffn_w1.rearrange("(k p) n -> p k n", p=P)).then_inc(s("ld_w1"), 16)
            sp.dma_start(w2_raw, ffn_w2.rearrange("(m p) n -> p m n", p=P)).then_inc(s("ld_w2"), 16)
            for b in range(B):
                sp.wait_ge(s("fin"), b + 1)
                sp.dma_start(out[b], xm[:, b, :]).then_inc(s("out"), 16)
            sp.wait_ge(s("out"), 16 * B)

        def heads_cols(t, j):
            return t[:, :, 0:2, j * DH:(j + 1) * DH]

        @blk.gpsimd
        def _(pool):
            pool.wait_ge(s("var1"), 1)
            pool.tensor_tensor(rstd[:, :], veps[:, :], pw[:, :], ALU.pow).then_inc(s("rstd1"), 1)

            def split_v(g):
                pool.wait_ge(s_wraw[g % 2], 32 * (g // 2 + 1))
                if g >= 2:
                    pool.wait_ge(s("p"), proj_no[("v", 2 * (g - 2) + 1, CH - 1)] + 1)
                src = w_raw[g % 2][:, :, 2, :]
                pool.tensor_copy(w_v_h[:, g % 2, :, :], src).then_inc(s("wh"), 1)
                pool.wait_ge(s("wh"), 5 * g + 1)
                pool.tensor_tensor(w_v_l[:, g % 2, :, :], src, w_v_h[:, g % 2, :, :].bitcast(F32), ALU.subtract)\
                    .then_inc(s("wsplit"), 1)

            def split_qk(g, j):
                if g >= 1:
                    pool.wait_ge(s("p"), proj_no[("k", (2 * (g - 1) + 1) * HPG + j)] + 1)
                src = heads_cols(w_raw[g % 2], j)
                for k in range(KT):
                    last = pool.tensor_copy(heads_cols(w_qk_h, j)[:, k, :, :], src[:, k, :, :])
                last.then_inc(s("wh"), 1)
                pool.wait_ge(s("wh"), 5 * g + 2 + j)
                for k in range(KT):
                    last = pool.tensor_tensor(heads_cols(w_qk_l, j)[:, k, :, :], src[:, k, :, :],
                                              heads_cols(w_qk_h, j)[:, k, :, :].bitcast(F32), ALU.subtract)
                last.then_inc(s("wsplit"), 1)

            split_v(0)
            for j in range(HPG):
                split_qk(0, j)
            for g in range(GROUPS):
                hs = slice(g * HPG, (g + 1) * HPG)
                raw = ow_raw[g % 2][:, :, :]
                pool.wait_ge(s(f"ld_ow{g % 2}"), 16 * (g // 2 + 1))
                pool.tensor_copy(ow_h[:, hs, :], raw).then_inc(s("owh"), 1)
                pool.wait_ge(s("owh"), g + 1)
                pool.tensor_tensor(ow_l[:, hs, :], raw, ow_h[:, hs, :].bitcast(F32), ALU.subtract)\
                    .then_inc(s("ow"), 1)
                if g + 1 < GROUPS:
                    split_v(g + 1)
                    for j in range(HPG):
                        split_qk(g + 1, j)
            pool.wait_ge(s("p"), len(order))
            pool.wait_ge(s("ld_w1"), 16)
            pool.tensor_copy(w1_h, w1_raw).then_inc(s("ffw"), 1)
            pool.wait_ge(s("ffw"), 1)
            pool.tensor_tensor(w1_l, w1_raw, w1_h.bitcast(F32), ALU.subtract).then_inc(s("ffw"), 1)
            pool.wait_ge(s("ld_w2"), 16)
            pool.tensor_copy(w2_h, w2_raw).then_inc(s("ffw"), 1)
            pool.wait_ge(s("ffw"), 3)
            pool.tensor_tensor(w2_l, w2_raw, w2_h.bitcast(F32), ALU.subtract).then_inc(s("ffw"), 1)
            pool.wait_ge(s("var2"), 1)
            pool.tensor_tensor(rstd[:, :], veps[:, :], pw[:, :], ALU.pow).then_inc(s("rstd2"), 1)

        def three(pe, dst, ah, al, bh, bl, start, stop):
            pe.matmul(dst, al, bh, start=start, stop=False)
            pe.matmul(dst, ah, bl, start=False, stop=False)
            return pe.matmul(dst, ah, bh, start=False, stop=stop)

        @blk.tensor
        def _(pe):
            pe.wait_ge(s_ld["small1"], 128)
            pe.wait_ge(s_ld["ada"], 32)
            ada_raw = w_raw[1][:, :, :, :].rearrange("p k s n -> p k (s n)")
            pe.wait_ge(s("xm"), B)
            for i, col in enumerate((0, 1, 2, 3, 6, 7, 8, 9)):
                for k in range(KT):
                    mm = pe.matmul(bank_g[:, i * B:(i + 1) * B], ada_raw[:, k, col * P:(col + 1) * P],
                                   temb_t[:, k, :], start=(k == 0), stop=(k == KT - 1))
            for k in range(KT):
                mm = pe.matmul(bank_o1[0:B, :].rearrange("p (g n) -> p g n", g=2), temb_t[:, k, :],
                               ada_raw[:, k, :].rearrange("p (h g n) -> p h g n", h=2, g=3)[:, :, 2, :],
                               start=(k == 0), stop=(k == KT - 1))
            mm.then_inc(s("ada"), 1)

            def ln_transposes(name, b):
                pe.wait_ge(s("xn" + name), b + 1)
                if b >= 2:
                    pe.wait_ge(s("xf" + name), b - 1)
                for k in range(KT):
                    mm = pe.transpose(bank_p[b % 2][:, k * P:(k + 1) * P], xn[:, b % 2, k * P:(k + 1) * P],
                                      ident[:, :])
                mm.then_inc(s("xt" + name), 1)

            for b in range(B):
                ln_transposes("1", b)

            def take_bank(i):
                if i >= 2:
                    pe.wait_ge(s("pe"), i - 1)
                elif i == 0:
                    pe.wait_ge(s("xh1"), B)
                    pe.wait_ge(s("xl1"), B)

            def project_v(m, k):
                i = proj_no[("v", m, k)]
                take_bank(i)
                g, c = divmod(m, 2)
                b = c * CH + k
                if k == 0 and c == 0:
                    pe.wait_ge(s("wsplit"), 5 * g + 1)
                for t in range(KT):
                    mm = three(pe, bank_p[i % 2][:, :], xh[:, t, b * D:(b + 1) * D], xl[:, t, b * D:(b + 1) * D],
                               w_v_h[:, g % 2, t, :], w_v_l[:, g % 2, t, :], t == 0, t == KT - 1)
                mm.then_inc(s("p"), 1)

            def project_qk(n):
                m, j, g, c = part(n)
                if c == 0:
                    pe.wait_ge(s("wsplit"), 5 * g + 2 + j)
                for w, name in enumerate("qk"):
                    i = proj_no[(name, n)]
                    take_bank(i)
                    for t in range(KT):
                        cols = slice(j * DH, (j + 1) * DH)
                        mm = three(pe, bank_p[i % 2][:, :], w_qk_h[:, t, w, cols], w_qk_l[:, t, w, cols],
                                   xh[:, t, c * CT:(c + 1) * CT], xl[:, t, c * CT:(c + 1) * CT],
                                   t == 0, t == KT - 1)
                    mm.then_inc(s("p"), 1)

            def scores(n):
                pe.wait_ge(s("pe"), proj_no[("k", n)] + 1)
                if n >= 2:
                    pe.wait_ge(s("exp1"), n - 1)
                for b in range(CH):
                    mm = pe.matmul(bank_s1[n % 2][:, b * D:(b + 1) * D], qk[:, n % 2, 0, b * D:(b + 1) * D],
                                   qk[:, n % 2, 1, b * D:(b + 1) * D], start=True, stop=True)
                mm.then_inc(s("s1"), 1)

            def turn_probs(n):
                pe.wait_ge(s("norm"), n + 1)
                if n >= 1:
                    pe.wait_ge(s("pt1"), n)
                for b in range(CH):
                    mm = pe.transpose(bank_t1[:, b * D:(b + 1) * D], prob[:, n % 2, b, :], ident[:, :])
                mm.then_inc(s("t1"), 1)

            def attend(n):
                m, j, g, c = part(n)
                pe.wait_ge(s("pt1"), n + 1)
                pe.wait_ge(s("pe"), proj_no[("v", m, CH - 1)] + 1)
                if n >= 1:
                    pe.wait_ge(s("atl"), n)
                for b in range(CH):
                    mm = pe.matmul(bank_v1[:, b * D:(b + 1) * D], v_sb[:, m % 2, b, j * DH:(j + 1) * DH],
                                   prob_t[:, n % 2, b, :], start=True, stop=True)
                mm.then_inc(s("av"), 1)

            def out_project(m, k):
                g, c = divmod(m, 2)
                i = m * CH + k
                pe.wait_ge(s("atl"), HPG * (m + 1))
                pe.wait_ge(s("ath"), HPG * (m + 1))
                pe.wait_ge(s("ow"), g + 1)
                if i >= 1:
                    pe.wait_ge(s("acc"), i)
                else:
                    pe.wait_ge(s("mod"), 1)
                cols = slice(k * D, (k + 1) * D)
                for j in range(HPG):
                    mm = three(pe, bank_o1[:, 0:DIM], at_h[:, c, j, cols], at_l[:, c, j, cols],
                               ow_h[:, g * HPG + j, :], ow_l[:, g * HPG + j, :], j == 0, j == HPG - 1)
                mm.then_inc(s("op"), 1)

            for k in range(CH):
                project_v(0, k)
            project_qk(0)
            for n in range(STEPS):
                m, k, g, c = part(n)
                scores(n)
                if n >= 1:
                    attend(n - 1)
                if n + 1 < STEPS:
                    project_qk(n + 1)
                turn_probs(n)
                if m + 1 < HGROUPS:
                    project_v(m + 1, k)
                if m >= 1:
                    out_project(m - 1, k)
            attend(STEPS - 1)
            for k in range(CH):
                out_project(HGROUPS - 1, k)

            def spread_gates(i, b):
                pe.wait_ge(s("mod"), 1)
                if i >= 1:
                    pe.wait_ge(s("gate"), i)
                pe.matmul(bank_g[:, :].rearrange("p (g n) -> p g n", g=2), sel[:, b, :], gates[:, :, :],
                          start=True, stop=True).then_inc(s("g"), 1)

            for b in range(B):
                spread_gates(b, b)
            for b in range(B):
                ln_transposes("2", b)
            pe.wait_ge(s("xh2"), B)
            pe.wait_ge(s("xl2"), B)
            pe.wait_ge(s("ffw"), 4)
            for c in range(2):
                for mb in range(MB):
                    i = c * MB + mb
                    if i >= 2:
                        pe.wait_ge(s("gelu"), i - 1)
                    for t in range(KT):
                        cols = slice(mb * P, (mb + 1) * P)
                        mm = three(pe, bank_p[i % 2][:, :], w1_h[:, t, cols], w1_l[:, t, cols],
                                   xh[:, t, c * CT:(c + 1) * CT], xl[:, t, c * CT:(c + 1) * CT],
                                   t == 0, t == KT - 1)
                    mm.then_inc(s("f1"), 1)
                for k in range(CH):
                    b = c * CH + k
                    pe.wait_ge(s("hl"), MB * (c + 1))
                    if b >= 2:
                        pe.wait_ge(s("y"), b - 1)
                    spread_gates(B + b, b)
                    for mb in range(MB):
                        cols = slice(k * D, (k + 1) * D)
                        mm = three(pe, bank_s1[b % 2][:, 0:DIM], h_h[:, mb, cols], h_l[:, mb, cols],
                                   w2_h[:, mb, :], w2_l[:, mb, :], mb == 0, mb == MB - 1)
                    mm.then_inc(s("f2"), 1)

        @blk.scalar
        def _(act):
            def ln_high(name, b, shift):
                act.wait_ge(s("xt" + name), b + 1)
                act.wait_ge(s("mod"), 1)
                if name == "2" and b == 0:
                    act.wait_ge(s("p"), len(order))
                if b >= 2:
                    act.wait_ge(s("xl" + name), b - 1)
                for k in range(KT):
                    last = act.activation(xn_f[:, b % 2, k, :], bank_p[b % 2][:, k * P:(k + 1) * P],
                                          ACT.Identity, bias=mod[:, shift + k, b:b + 1],
                                          scale=mod[:, shift + 2 + k, b:b + 1])
                last.then_inc(s("xf" + name), 1)
                act.wait_ge(s("xf" + name), b + 1)
                act.activation(xh[:, :, b * D:(b + 1) * D], xn_f[:, b % 2, :, :], ACT.Copy)\
                    .then_inc(s("xh" + name), 1)

            for b in range(B):
                ln_high("1", b, 0)

            def evacuate_v(m, k):
                i = proj_no[("v", m, k)]
                act.wait_ge(s("p"), i + 1)
                if m >= 2:
                    act.wait_ge(s("av"), HPG * (m - 1))
                act.activation(v_sb[:, m % 2, k, :], bank_p[i % 2][:, :], ACT.Copy).then_inc(s("pe"), 1)

            def evacuate_qk(n):
                m, j, g, c = part(n)
                for w, name in enumerate("qk"):
                    i = proj_no[(name, n)]
                    act.wait_ge(s("p"), i + 1)
                    if n >= 2:
                        act.wait_ge(s("s1"), n - 1)
                    h = g * HPG + j
                    bias = q_bias[:, h:h + 1] if w == 0 else qkv_bt[:, NH1 + h:NH1 + h + 1]
                    act.activation(qk[:, n % 2, w, :], bank_p[i % 2][:, :], ACT.Identity, bias=bias,
                                   scale=SCALE1 if w == 0 else 1.0).then_inc(s("pe"), 1)

            def attention_high(n):
                m, j, g, c = part(n)
                h = g * HPG + j
                act.wait_ge(s("av"), n + 1)
                if m >= 2:
                    act.wait_ge(s("op"), CH * (m - 1))
                act.activation(at_h[:, c, j, :], bank_v1[:, :], ACT.Identity,
                               bias=qkv_bt[:, 2 * NH1 + h:2 * NH1 + h + 1], scale=1.0).then_inc(s("ath"), 1)

            for k in range(CH):
                evacuate_v(0, k)
            evacuate_qk(0)
            for n in range(STEPS):
                m, k, g, c = part(n)
                act.wait_ge(s("max1"), n + 1)
                if n >= 2:
                    act.wait_ge(s("t1"), n - 1)
                    act.wait_ge(s("rs1"), n - 1)
                for b in range(CH):
                    last = act.activation(prob[:, n % 2, b, :], bank_s1[n % 2][:, b * D:(b + 1) * D], ACT.Exp,
                                          bias=nm1[:, n % 2, b:b + 1], scale=1.0,
                                          accum_out=sum1[:, n % 2, b:b + 1])
                last.then_inc(s("exp1"), 1)
                if n >= 1:
                    attention_high(n - 1)
                if n + 1 < STEPS:
                    evacuate_qk(n + 1)
                if m + 1 < HGROUPS:
                    evacuate_v(m + 1, k)
            attention_high(STEPS - 1)
            for b in range(B):
                ln_high("2", b, 4)
            for c in range(2):
                for mb in range(MB):
                    i = c * MB + mb
                    act.wait_ge(s("f1"), i + 1)
                    if c == 1:
                        act.wait_ge(s("hl"), mb + 1)
                    act.activation(h_f[:, mb, :], bank_p[i % 2][:, :], ACT.Gelu, bias=b1_t[:, mb:mb + 1], scale=1.0)\
                       .then_inc(s("gelu"), 1)
                    act.wait_ge(s("gelu"), i + 1)
                    if c == 1:
                        act.wait_ge(s("f2"), CH)
                    act.activation(h_h[:, mb, :], h_f[:, mb, :], ACT.Copy).then_inc(s("hh"), 1)

        @blk.vector
        def _(dve):
            def ln_stats(name, src, ready):
                for b in range(B):
                    if ready is not None:
                        dve.wait_ge(ready, b + 1)
                    dve.bn_stats(stats[:, b, :], src[:, b, :]).then_inc(s("st" + name), 1)
                    dve.wait_ge(s("st" + name), b + 1)
                    last = dve.bn_aggr(mv[:, b, :], stats[:, b, :])
                last.then_inc(s("mv" + name), 1)
                dve.wait_ge(s("mv" + name), 1)
                dve.tensor_scalar(veps[:, :], mv[:, :, 1], LN_EPS, None, ALU.add).then_inc(s("var" + name), 1)

            def ln_tokens(name, src):
                dve.wait_ge(s("rstd" + name), 1)

                def normal(b):
                    if b >= 2:
                        dve.wait_ge(s("xt" + name), b - 1)
                    dve.tensor_scalar(xn[:, b % 2, :], src[:, b, :], mv[:, b, 0:1], rstd[:, b:b + 1],
                                      ALU.subtract, ALU.mult).then_inc(s("xn" + name), 1)

                normal(0)
                for b in range(B):
                    if b + 1 < B:
                        normal(b + 1)
                    dve.wait_ge(s("xh" + name), b + 1)
                    dve.tensor_tensor(xl[:, :, b * D:(b + 1) * D], xn_f[:, b % 2, :, :],
                                      xh[:, :, b * D:(b + 1) * D].bitcast(F32), ALU.subtract)\
                       .then_inc(s("xl" + name), 1)

            ln_stats("1", xm, s("xm"))
            dve.wait_ge(s("ada"), 1)
            dve.tensor_tensor(mod[:, 0:4, :], bank_g[:, 0:4 * B].rearrange("p (i b) -> p i b", b=B),
                              ada_bt[:, 0:4].unsqueeze(2).to_broadcast([P, 4, B]), ALU.add)
            dve.tensor_tensor(mod[:, 4:8, :], bank_g[:, 4 * B:8 * B].rearrange("p (i b) -> p i b", b=B),
                              ada_bt[:, 6:10].unsqueeze(2).to_broadcast([P, 4, B]), ALU.add).then_inc(s("mod0"), 1)
            dve.tensor_tensor(gates[:, :, :], bank_o1[0:B, :].rearrange("p (g n) -> p g n", g=2), gate_b[:, :, :],
                              ALU.add)
            dve.tensor_scalar(q_bias[:, :], qkv_bt[:, 0:NH1], SCALE1, None, ALU.mult)
            dve.wait_ge(s("mod0"), 1)
            dve.tensor_scalar(mod[:, :, :].rearrange("p (l i) b -> p l i b", l=2)[:, :, 2:4, :],
                              mod[:, :, :].rearrange("p (l i) b -> p l i b", l=2)[:, :, 2:4, :],
                              1.0, None, ALU.add).then_inc(s("mod"), 1)
            dve.wait_ge(s("mod"), 1)
            ln_tokens("1", xm)

            def attention_low(n):
                m, j, g, c = part(n)
                h = g * HPG + j
                dve.wait_ge(s("ath"), n + 1)
                dve.scalar_tensor_tensor(out=at_l[:, c, j, :], in0=bank_v1[:, :],
                                         scalar=qkv_bt[:, 2 * NH1 + h:2 * NH1 + h + 1],
                                         in1=at_h[:, c, j, :].bitcast(F32), op0=ALU.add, op1=ALU.subtract)\
                   .then_inc(s("atl"), 1)

            def accumulate(m, k):
                g, c = divmod(m, 2)
                b = c * CH + k
                dve.wait_ge(s("op"), m * CH + k + 1)
                if g >= 1:
                    dve.wait_ge(s("acc"), (m - 2) * CH + k + 1)
                dve.tensor_tensor(acc[:, b, :], bank_o1[:, 0:DIM], out_b_bc[:, :] if g == 0 else acc[:, b, :],
                                  ALU.add).then_inc(s("acc"), 1)

            for n in range(STEPS):
                m, k, g, c = part(n)
                dve.wait_ge(s("s1"), n + 1)
                dve.tensor_reduce(nm1[:, n % 2, :], bank_s1[n % 2][:, :].rearrange("p (b t) -> p b t", b=CH),
                                  AX.X, ALU.max, negate=True).then_inc(s("max1"), 1)
                dve.wait_ge(s("exp1"), n + 1)
                dve.reciprocal(rs1[:, n % 2, :], sum1[:, n % 2, :]).then_inc(s("rs1"), 1)
                dve.wait_ge(s("rs1"), n + 1)
                dve.tensor_tensor(prob[:, n % 2, :, :], prob[:, n % 2, :, :],
                                  rs1[:, n % 2, :].unsqueeze(2).to_broadcast([P, CH, D]), ALU.mult)\
                   .then_inc(s("norm"), 1)
                if n >= 1:
                    attention_low(n - 1)
                dve.wait_ge(s("t1"), n + 1)
                if n >= 2:
                    dve.wait_ge(s("av"), n - 1)
                dve.tensor_copy(prob_t[:, n % 2, :, :].rearrange("p b t -> p (b t)"), bank_t1[:, :])\
                   .then_inc(s("pt1"), 1)
                if m >= 1:
                    accumulate(m - 1, k)
            attention_low(STEPS - 1)
            for k in range(CH):
                accumulate(HGROUPS - 1, k)
            for b in range(B):
                dve.wait_ge(s("g"), b + 1)
                dve.wait_ge(s("acc"), (HGROUPS - 2) * CH + b + 1)
                dve.tensor_tensor(acc[:, b, :], acc[:, b, :], bank_g[:, 0:DIM], ALU.mult).then_inc(s("gate"), 1)
                dve.wait_ge(s("gate"), b + 1)
                dve.tensor_tensor(acc[:, b, :], acc[:, b, :], xm[:, b, :], ALU.add).then_inc(s("res"), 1)
            ln_stats("2", acc, s("res"))
            for b in range(B):
                last = dve.tensor_tensor(xm[:, b, :], xm[:, b, :], acc[:, b, :], ALU.add)
            last.then_inc(s("base"), 1)
            dve.wait_ge(s("base"), 1)
            ln_tokens("2", acc)
            for c in range(2):
                for mb in range(MB):
                    i = c * MB + mb
                    dve.wait_ge(s("hh"), i + 1)
                    dve.tensor_tensor(h_l[:, mb, :], h_f[:, mb, :], h_h[:, mb, :].bitcast(F32), ALU.subtract)\
                       .then_inc(s("hl"), 1)
                for k in range(CH):
                    b = c * CH + k
                    dve.wait_ge(s("f2"), b + 1)
                    dve.tensor_tensor(acc[:, b, :], bank_s1[b % 2][:, 0:DIM], b2_bc[:, :], ALU.add).then_inc(s("y"), 1)
                    dve.wait_ge(s("y"), b + 1)
                    dve.wait_ge(s("g"), B + b + 1)
                    dve.tensor_tensor(acc[:, b, :], acc[:, b, :], bank_g[:, DIM:2 * DIM], ALU.mult)\
                       .then_inc(s("gate"), 1)
                    dve.wait_ge(s("gate"), B + b + 1)
                    dve.tensor_tensor(xm[:, b, :], xm[:, b, :], acc[:, b, :], ALU.add).then_inc(s("fin"), 1)

        ctx2.close()


_INPUTS = ["x", "cond", "cond_t", "wq_t", "wo_t", "ada_w", "ada_b", "ada_b_t", "qkv_w", "qkv_b_t", "out_w", "out_b",
           "ffn_w1", "ffn_b1_t", "ffn_w2", "ffn_b2", "roles"]


def lay_out(inputs):
    import numpy as np
    c = np.ascontiguousarray
    i = {k: np.asarray(v) for k, v in inputs.items()}
    return {
        "x": i["x"], "cond": i["cond_2048"], "cond_t": c(i["cond_2048"].T),
        "wq_t": c(i["L0_cond_Wq"].T), "wo_t": c(i["L0_cond_Wo"].T),
        "ada_w": i["L1_cond_ada_w"], "ada_b": i["L1_cond_ada_b"],
        "ada_b_t": c(i["L1_cond_ada_b"].reshape(12, P).T),
        "qkv_w": i["L1_cond_qkv_w"], "qkv_b_t": c(i["L1_cond_qkv_b"].reshape(3 * NH1, DH).T),
        "out_w": i["L1_cond_out_w"], "out_b": i["L1_cond_out_b"],
        "ffn_w1": i["L1_cond_ffn_w1"], "ffn_b1_t": c(i["L1_cond_ffn_b1"].reshape(MB, P).T),
        "ffn_w2": i["L1_cond_ffn_w2"], "ffn_b2": i["L1_cond_ffn_b2"], "roles": row_roles(),
    }


def kernel(**inputs):
    import numpy as np
    import concourse.bacc as bacc
    from concourse.bass_utils import run_bass_kernel_spmd

    nc = bacc.Bacc("TRN2", target_bir_lowering=False, num_devices=1)
    arrays = lay_out(inputs)
    aps = {n: nc.dram_tensor(n + "_dram", a.shape, mybir.dt.from_np(a.dtype), kind="ExternalInput").ap()
           for n, a in arrays.items()}
    aps["out"] = nc.dram_tensor("out_dram", (B, D, DIM), F32, kind="ExternalOutput").ap()
    build_program(nc, **aps)
    result = run_bass_kernel_spmd(nc, [{n + "_dram": a for n, a in arrays.items()}], core_ids=[0])
    return result.results[0]["out_dram"]
```

```python
from contextlib import ExitStack

import concourse.bass as bass
from concourse import mybir

F32 = mybir.dt.float32
F32R = mybir.dt.float32r
ALU = mybir.AluOpType
ACT = mybir.ActivationFunctionType
AX = mybir.AxisListType

P = 128
B = 8
T = 256
D = 128
NH0, DK = 8, 16
NH1, DH = 16, 128
DIM, INNER, MLP = T, NH1 * DH, 4 * T
KT = DIM // P
NEG = 1e30
LN_EPS = 1e-6
SCALE1 = float(DH) ** -0.5

HEAD_ROWS = 64
MASK_ROW = 3 * DK
MAX_ROW = MASK_ROW + 3
PAIRS = NH0 // 2
HPG = 4
GROUPS = NH1 // HPG
CH = B // 2
CT = CH * D
STEPS = GROUPS * 2 * HPG
MB = MLP // P
EARLY = {(7, 1): 0, (7, 3): 1, (7, 5): 2, (7, 7): 3, (8, 3): 4, (9, 0): 5}


def row_roles():
    import numpy as np
    t = np.zeros((P, 7), np.float32)
    t[1, 4] = -1.0
    for i in range(2):
        o = i * HEAD_ROWS
        t[o:o + 3 * DK, 2] = 0.25
        t[o + DK:o + 2 * DK, 1] = -1.0
        t[o + 2 * DK:o + 3 * DK, 0] = -1.0
        t[o + MASK_ROW:o + MASK_ROW + 3, 2] = NEG
        t[o + MASK_ROW:o + MASK_ROW + 3, 3] = -NEG
        t[o + MASK_ROW + 1, 1] = -1.0
        t[o + MASK_ROW + 2, 0] = -1.0
        t[o + MAX_ROW:o + MAX_ROW + 2, 3] = 1.0
    t[:, 5:7] = t[:, 1:2] * t[:, 2:4]
    return t


def build_program(nc, x, cond, cond_t, wq_t, wo_t, ada_w, ada_b, ada_b_t, qkv_w, qkv_b_t, out_w, out_b,
                  ffn_w1, ffn_b1_t, ffn_w2, ffn_b2, roles, out):
    ctx = ExitStack()
    with ctx:
        def sb(name, shape, dt=F32):
            return ctx.enter_context(nc.sbuf_tensor(name, shape, dt))

        def sem(name):
            return ctx.enter_context(nc.semaphore(name))

        ident = sb("ident", [P, P])
        role = sb("role", [P, 7])
        temb_t = sb("temb_t", [P, KT, B])
        ada_bt = sb("ada_bt", [P, 12])
        gate_b = sb("gate_b", [B, 2, DIM])
        qkv_bt = sb("qkv_bt", [P, 3 * NH1])
        q_bias = sb("q_bias", [P, NH1])
        b1_t = sb("b1_t", [P, MB])
        out_b_bc = sb("out_b_bc", [P, DIM])
        b2_bc = sb("b2_bc", [P, DIM])
        mod = sb("mod", [P, 8, B])
        gates = sb("gates", [B, 2, DIM])
        sel = sb("sel", [B, B, P])
        pw = sb("pw", [P, B])
        stats = sb("stats", [P, B, 6])
        mv = sb("mv", [P, B, 2])
        veps = sb("veps", [P, B])
        rstd = sb("rstd", [P, B])
        xm = sb("xm", [P, B, DIM])
        acc = sb("acc", [P, B, DIM])
        xh = sb("xh", [P, KT, B * D], F32R)
        xl = sb("xl", [P, KT, B * D], F32R)
        xn = sb("xn", [P, 2, DIM])
        xn_f = sb("xn_f", [P, 2, KT, D])
        v_sb = sb("v_sb", [P, 2, CH, HPG * DH])
        qk = sb("qk", [P, 2, 2, CT])
        w_raw = [sb(f"w_raw{i}", [P, KT, 3, HPG * DH]) for i in range(2)]
        w_qk_h = sb("w_qk_h", [P, KT, 2, HPG * DH], F32R)
        w_qk_l = sb("w_qk_l", [P, KT, 2, HPG * DH], F32R)
        w_v_h = sb("w_v_h", [P, 2, KT, HPG * DH], F32R)
        w_v_l = sb("w_v_l", [P, 2, KT, HPG * DH], F32R)

        banks = [ctx.enter_context(nc.psum_tensor(f"bank{i}", [P, 512], F32)) for i in range(8)]
        s_xin = [sem(f"s_xin{b}") for b in range(B)]
        s_ld = {k: sem("s_ld_" + k) for k in ("small0", "cond", "wq", "wo", "small1", "ada")}
        s_wraw = [sem(f"s_wraw{i}") for i in range(2)]
        S = {}

        def s(name):
            if name not in S:
                S[name] = sem("s_" + name)
            return S[name]

        def three(pe, dst, ah, al, bh, bl, start, stop):
            pe.matmul(dst, al, bh, start=start, stop=False)
            pe.matmul(dst, ah, bl, start=False, stop=False)
            return pe.matmul(dst, ah, bh, start=False, stop=stop)

        def ln_stats(dve, name, b, src):
            dve.bn_stats(stats[:, b, :], src[:, b, :]).then_inc(s("st" + name), 1)
            dve.wait_ge(s("st" + name), b + 1)
            dve.bn_aggr(mv[:, b, :], stats[:, b, :]).then_inc(s("mv" + name), 1)

        def ln_rstd(pool, name, b):
            pool.wait_ge(s("mv" + name), b + 1)
            pool.tensor_scalar(veps[:, b:b + 1], mv[:, b, 1:2], LN_EPS, None, ALU.add).then_inc(s("var" + name), 1)
            pool.wait_ge(s("var" + name), b + 1)
            pool.tensor_tensor(rstd[:, b:b + 1], veps[:, b:b + 1], pw[:, b:b + 1], ALU.pow)\
                .then_inc(s("rstd" + name), 1)

        def ln_normal(dve, name, b, src):
            dve.wait_ge(s("rstd" + name), b + 1)
            if b >= 2:
                dve.wait_ge(s("xt" + name), b - 1)
            dve.tensor_scalar(xn[:, b % 2, :], src[:, b, :], mv[:, b, 0:1], rstd[:, b:b + 1],
                              ALU.subtract, ALU.mult).then_inc(s("xn" + name), 1)

        def ln_transposes(pe, name, b, bank):
            pe.wait_ge(s("xn" + name), b + 1)
            for k in range(KT):
                mm = pe.transpose(bank[:, k * P:(k + 1) * P], xn[:, b % 2, k * P:(k + 1) * P], ident[:, :])
            mm.then_inc(s("xt" + name), 1)

        def ln_modulate(act, name, b, bank, shift):
            act.wait_ge(s("xt" + name), b + 1)
            if b == 0:
                act.wait_ge(s("mod"), 1)
            if b >= 2:
                act.wait_ge(s("xl" + name), b - 1)
            for k in range(KT):
                last = act.activation(xn_f[:, b % 2, k, :], bank[:, k * P:(k + 1) * P], ACT.Identity,
                                      bias=mod[:, shift + k, b:b + 1], scale=mod[:, shift + 2 + k, b:b + 1])
            last.then_inc(s("xf" + name), 1)
            act.wait_ge(s("xf" + name), b + 1)
            act.activation(xh[:, :, b * D:(b + 1) * D], xn_f[:, b % 2, :, :], ACT.Copy).then_inc(s("xh" + name), 1)

        def ln_low(dve, name, b):
            dve.wait_ge(s("xh" + name), b + 1)
            dve.tensor_tensor(xl[:, :, b * D:(b + 1) * D], xn_f[:, b % 2, :, :],
                              xh[:, :, b * D:(b + 1) * D].bitcast(F32), ALU.subtract).then_inc(s("xl" + name), 1)

        def heads_cols(t, j):
            return t[:, :, 0:2, j * DH:(j + 1) * DH]

        HGROUPS = 2 * GROUPS

        def part(n):
            m, k = divmod(n, HPG)
            return m, k, m // 2, m % 2

        proj_no = {}
        order = [("v", 0, k) for k in range(CH)] + [("q", 0), ("k", 0)]
        for n in range(STEPS):
            m, k, hg, c = part(n)
            if n + 1 < STEPS:
                order += [("q", n + 1), ("k", n + 1)]
            if m + 1 < HGROUPS:
                order += [("v", m + 1, k)]
        for i, what in enumerate(order):
            proj_no[what] = i

        w1_raw = w_raw[0][:, :, :, :].rearrange("p k s n -> p (k s n)")[:, 0:KT * MLP]\
            .rearrange("p (k n) -> p k n", k=KT)
        w2_raw = w_raw[1][:, :, :, :].rearrange("p k s n -> p (k s n)")[:, 0:MB * DIM]\
            .rearrange("p (m n) -> p m n", m=MB)

        def split_v(pool, g):
            pool.wait_ge(s_wraw[g % 2], 32 * (g // 2 + 1))
            if g >= 2:
                pool.wait_ge(s("p"), proj_no[("v", 2 * (g - 2) + 1, CH - 1)] + 1)
            src = w_raw[g % 2][:, :, 2, :]
            pool.tensor_copy(w_v_h[:, g % 2, :, :], src).then_inc(s("wh"), 1)
            pool.wait_ge(s("wh"), 5 * g + 1)
            pool.tensor_tensor(w_v_l[:, g % 2, :, :], src, w_v_h[:, g % 2, :, :].bitcast(F32), ALU.subtract)\
                .then_inc(s("wsplit"), 1)

        def split_qk(pool, g, j):
            if g >= 1:
                pool.wait_ge(s("p"), proj_no[("k", (2 * (g - 1) + 1) * HPG + j)] + 1)
            if g < GROUPS:
                src = heads_cols(w_raw[g % 2], j)
            else:
                src = heads_cols(w1_raw.rearrange("p k (s n) -> p k s n", s=2), j)
            for k in range(KT):
                last = pool.tensor_copy(heads_cols(w_qk_h, j)[:, k, :, :], src[:, k, :, :])
            last.then_inc(s("wh"), 1)
            before = 5 * g + 1 if g < GROUPS else 5 * GROUPS
            pool.wait_ge(s("wh"), before + 1 + j)
            for k in range(KT):
                last = pool.tensor_tensor(heads_cols(w_qk_l, j)[:, k, :, :], src[:, k, :, :],
                                          heads_cols(w_qk_h, j)[:, k, :, :].bitcast(F32), ALU.subtract)
            last.then_inc(s("wsplit"), 1)

        def load_group(sp, g):
            for k in range(KT):
                sp.dma_start(w_raw[g % 2][:, k, :, :],
                             qkv_w[k * P:(k + 1) * P, :].rearrange("p (s n) -> p s n", s=3)
                             [:, :, g * HPG * DH:(g + 1) * HPG * DH]).then_inc(s_wraw[g % 2], 16)

        bank_p = banks[0:2]

        def take_bank(pe, i):
            if i >= 2:
                pe.wait_ge(s("pe"), i - 1)

        def project_v(pe, m, k):
            i = proj_no[("v", m, k)]
            take_bank(pe, i)
            g, c = divmod(m, 2)
            b = c * CH + k
            if k == 0 and c == 0:
                pe.wait_ge(s("wsplit"), 5 * g + 1)
            for t in range(KT):
                mm = three(pe, bank_p[i % 2][:, :], xh[:, t, b * D:(b + 1) * D], xl[:, t, b * D:(b + 1) * D],
                           w_v_h[:, g % 2, t, :], w_v_l[:, g % 2, t, :], t == 0, t == KT - 1)
            mm.then_inc(s("p"), 1)

        def project_qk(pe, n):
            m, j, g, c = part(n)
            if c == 0:
                pe.wait_ge(s("wsplit"), 5 * g + 2 + j)
            for w, name in enumerate("qk"):
                i = proj_no[(name, n)]
                take_bank(pe, i)
                for t in range(KT):
                    cols = slice(j * DH, (j + 1) * DH)
                    mm = three(pe, bank_p[i % 2][:, :], w_qk_h[:, t, w, cols], w_qk_l[:, t, w, cols],
                               xh[:, t, c * CT:(c + 1) * CT], xl[:, t, c * CT:(c + 1) * CT],
                               t == 0, t == KT - 1)
                mm.then_inc(s("p"), 1)

        def evacuate_v(act, m, k):
            i = proj_no[("v", m, k)]
            act.wait_ge(s("p"), i + 1)
            if m >= 2:
                act.wait_ge(s("av"), HPG * (m - 1))
            act.activation(v_sb[:, m % 2, k, :], bank_p[i % 2][:, :], ACT.Copy).then_inc(s("pe"), 1)

        def evacuate_qk(act, n):
            m, j, g, c = part(n)
            for w, name in enumerate("qk"):
                i = proj_no[(name, n)]
                act.wait_ge(s("p"), i + 1)
                if n >= 2:
                    act.wait_ge(s("s1"), n - 1)
                h = g * HPG + j
                bias = q_bias[:, h:h + 1] if w == 0 else qkv_bt[:, NH1 + h:NH1 + h + 1]
                act.activation(qk[:, n % 2, w, :], bank_p[i % 2][:, :], ACT.Identity, bias=bias,
                               scale=SCALE1 if w == 0 else 1.0).then_inc(s("pe"), 1)

        l0 = ExitStack()

        def sb0(name, shape, dt=F32):
            return l0.enter_context(nc.sbuf_tensor(name, shape, dt))

        x_in = sb0("x_in", [P, B, T])
        rbc = sb0("rbc", [P, B, T])
        c_rows = xm[0:2, :, :].rearrange("p b t -> p (b t)")
        c_hi = xh[0:2, :, :].rearrange("p k t -> p (k t)")
        r_rows = [t[0:2, 1, :, :].rearrange("p k (b t) -> p (k b) t", t=T) for t in (w_v_h, w_v_l)]
        e_rows = sb0("e_rows", [2, P], F32R)
        w_q = sb0("w_q", [P, P])
        w_rep = sb0("w_rep", [P, PAIRS, P])
        w_o = sb0("w_o", [P, P])
        ones_c = sb0("ones_c", [P, 2, 32])
        zr = acc[:, 0:PAIRS, :]
        xr = [acc[:, PAIRS + i, :] for i in range(2)]
        dinv, cn = acc[:, PAIRS + 2, :], acc[:, PAIRS + 3, :]
        zh = sb0("zh", [P, PAIRS, T], F32R)
        zrh = sb0("zrh", [P, PAIRS, T], F32R)
        left = [sb0(f"left{i}", [P, PAIRS, T], F32R) for i in range(2)]
        leftm = [sb0(f"leftm{i}", [P, PAIRS, T], F32R) for i in range(2)]
        right = [sb0(f"right{i}", [P, PAIRS, T], F32R) for i in range(3)]
        nmax = sb0("nmax", [P, NH0, 2])
        nmax_h = sb0("nmax_h", [P, NH0, 2], F32R)
        mx = sb0("mx", [P, 2, 2, 2, P])
        pt = sb0("pt", [P, NH0, 2, T])
        vp = [sb0(f"vp{i}", [P, 2, NH0, 32]) for i in range(2)]

        bank_z = banks[0:2]
        bank_a, bank_s = banks[2:4], banks[4:6]
        bank_c, bank_m = banks[6], banks[7]

        blk = l0.enter_context(nc.Block())

        @blk.sync
        def _(sp):
            sp.dma_start(w_q[:, :], wq_t).then_inc(s_ld["wq"], 16)
            sp.dma_start(c_rows, cond.rearrange("b t -> (b t)").partition_broadcast(2)).then_inc(s_ld["cond"], 16)
            for b in range(B):
                sp.dma_start(x_in[:, b, :], x[b]).then_inc(s_xin[b], 16)
                if b == 0:
                    sp.dma_start(rbc[:, :, :], cond.partition_broadcast(P)).then_inc(s_ld["cond"], 16)
                    sp.dma_start(role[:, :], roles).then_inc(s_ld["small0"], 16)
                if b == 1:
                    sp.dma_start(temb_t[:, :, :], cond_t.rearrange("(k p) b -> p k b", p=P)).then_inc(s_ld["small1"], 16)
                    sp.dma_start(ada_bt[:, :], ada_b_t).then_inc(s_ld["small1"], 16)
                    for g in range(2):
                        sp.dma_start(gate_b[:, g, :], ada_b[(3 * g + 2) * DIM:(3 * g + 3) * DIM].partition_broadcast(B))\
                          .then_inc(s_ld["small1"], 16)
                    sp.dma_start(qkv_bt[:, :], qkv_b_t).then_inc(s_ld["small1"], 16)
                    sp.dma_start(b1_t[:, :], ffn_b1_t).then_inc(s_ld["small1"], 16)
                    sp.dma_start(out_b_bc[:, :], out_b.partition_broadcast(P)).then_inc(s_ld["small1"], 16)
                    sp.dma_start(b2_bc[:, :], ffn_b2.partition_broadcast(P)).then_inc(s_ld["small1"], 16)
                    for k in range(KT):
                        sp.dma_start(w_raw[1][:, k, :, :].rearrange("p s n -> p (s n)"), ada_w[k * P:(k + 1) * P, :])\
                          .then_inc(s_ld["ada"], 16)
            for h in range(NH0):
                r = 32 * (h % 4) + 16 * (h // 4)
                sp.dma_start(w_o[r:r + DK, :], wo_t[h * DK:(h + 1) * DK, :]).then_inc(s_ld["wo"], 16)
            load_group(sp, 0)
            sp.wait_ge(s("ada"), 1)
            load_group(sp, 1)

        @blk.gpsimd
        def _(pool):
            pool.memset(w_rep[:, :, :], 0.0).then_inc(s("memset"), 1)
            pool.memset(e_rows[:, :].bitcast(F32), 0.0).then_inc(s("memset"), 1)
            pool.memset(ident[:, :], 0.0).then_inc(s("memset"), 1)
            pool.memset(mx[:, :, :, :, :], 0.0).then_inc(s("mx0"), 1)
            pool.memset(ones_c[:, :, :], 0.0).then_inc(s("memset"), 1)
            for i in range(2):
                pool.memset(vp[i][:, :, :, :], 0.0).then_inc(s("vp0"), 1)
            pool.memset(sel[:, :, :], 0.0).then_inc(s("memset"), 1)
            pool.memset(pw[:, :], -0.5).then_inc(s("pw"), 1)
            pool.wait_ge(s("memset"), 5)
            pool.memset(e_rows[:, :].bitcast(F32).rearrange("p (i r) -> p i r", i=2)[:, :, MASK_ROW:MASK_ROW + 3], 1.0)\
                .then_inc(s("const"), 1)
            for a in range(2):
                pool.memset(ones_c[:, a, 16 * a:16 * a + 16], 1.0).then_inc(s("const"), 1)
            pool.affine_select(out=ident[:, :], in_=ident[:, :], compare_op=ALU.not_equal, fill=1.0, base=0,
                               pattern=[[-1, P]], channel_multiplier=1).then_inc(s("const"), 1)
            pool.affine_select(out=sel[:, :, :], in_=sel[:, :, :], compare_op=ALU.not_equal, fill=1.0, base=0,
                               pattern=[[-1, B], [0, P]], channel_multiplier=1).then_inc(s("const"), 1)
            pool.wait_ge(s_ld["wq"], 16)
            for k in range(3):
                pool.tensor_copy(w_rep[:, :, :].rearrange("p g (i r) -> p (g i) r", i=2)[:, :, k * DK:(k + 1) * DK],
                                 w_q[:, :].rearrange("p (h e) -> p h e", e=DK)).then_inc(s("wrep"), 1)

            def masked_x(b):
                pool.wait_ge(s_xin[b], 16)
                if b == 0:
                    pool.wait_ge(s_ld["cond"], 32)
                if b >= 2:
                    pool.wait_ge(s("z"), 2 * (b - 1))
                pool.tensor_tensor(xr[b % 2][:, :], x_in[:, b, :], rbc[:, b, :], ALU.mult).then_inc(s("xr"), 1)

            def right_op(b, n):
                pool.wait_ge(s("zr"), 2 * b + n + 1)
                if b >= 3:
                    pool.wait_ge(s("s"), (b - 2) * NH0)
                two = slice(2 * n, 2 * n + 2)
                pool.tensor_tensor(right[b % 3][:, two, :], zr[:, two, :], zrh[:, two, :].bitcast(F32), ALU.add)\
                    .then_inc(s("right"), 1)

            pool.wait_ge(s_ld["small0"], 16)
            for b in range(2):
                masked_x(b)
            for b in range(2):
                right_op(0, b)
            pieces = [lambda: split_v(pool, 0)] + [lambda j=j: split_qk(pool, 0, j) for j in range(HPG)]
            for b in range(-1, B + 2):
                if b + 3 < B:
                    masked_x(b + 3)
                if b + 2 < B:
                    right_op(b + 2, 0)
                if 1 <= b <= B:
                    ln_rstd(pool, "1", b - 1)
                if b + 2 < B:
                    right_op(b + 2, 1)
                if b >= 1 and pieces:
                    pieces.pop(0)()

        @blk.tensor
        def _(pe):
            def queries(b, n):
                pe.wait_ge(s("xr"), b + 1)
                if b >= 1:
                    pe.wait_ge(s("left"), 2 * b - 1 + n)
                    pe.wait_ge(s("zr"), 2 * b - 1 + n)
                pe.matmul(bank_z[n][:, :], e_rows[:, :],
                          r_rows[b // CH][:, b % CH, :].unsqueeze(1).to_broadcast([2, 2, T]), start=True, stop=False)
                for i in range(2):
                    mm = pe.matmul(bank_z[n][:, i * T:(i + 1) * T], w_rep[:, 2 * n + i, :], xr[b % 2][:, :],
                                   start=False, stop=(i == 1))
                mm.then_inc(s("z"), 1)

            def values(b):
                pe.wait_ge(s_xin[b], 16)
                pe.wait_ge(s("leftm"), 2 * b + 1)
                for k in range(2):
                    mm = pe.matmul(bank_m[:, k * P:(k + 1) * P], x_in[:, b, k * P:(k + 1) * P], w_q[:, :],
                                   start=True, stop=True)
                mm.then_inc(s("v"), 1)

            def scores_qk(b, h):
                n = b * NH0 + h
                if n >= 2:
                    pe.wait_ge(s("max"), n - 1)
                g, o = h // 2, HEAD_ROWS * (h % 2)
                for k in range(2):
                    mm = pe.matmul(bank_a[n % 2][:, k * T:(k + 1) * T],
                                   left[b % 2][o:o + MAX_ROW, g, k * P:(k + 1) * P],
                                   right[b % 3][o:o + MAX_ROW, g, :], start=True, stop=True)
                mm.then_inc(s("a"), 1)

            def scores_kq(b, h):
                n = b * NH0 + h
                if n >= 2:
                    pe.wait_ge(s("exp"), n - 1)
                g, o = h // 2, HEAD_ROWS * (h % 2)
                for k in range(2):
                    mm = pe.matmul(bank_s[n % 2][:, k * T:(k + 1) * T],
                                   right[b % 3][o:o + MAX_ROW + 2, g, k * P:(k + 1) * P],
                                   leftm[b % 2][o:o + MAX_ROW + 2, g, :], start=True, stop=True)
                mm.then_inc(s("s"), 1)

            def max_rows(b, half):
                n = 2 * b + half
                pe.wait_ge(s("mx"), n + 1)
                if half == 0:
                    if b >= 1:
                        pe.wait_ge(s("leftm"), n)
                    if b >= 3:
                        pe.wait_ge(s("xf1"), b - 2)
                else:
                    pe.wait_ge(s("vp"), b + 1)
                for g in range(2):
                    for k in range(2):
                        mm = pe.transpose(bank_m[:, (2 * g + k) * P:(2 * g + k + 1) * P],
                                          mx[:, half, k, g, :], ident[:, :])
                mm.then_inc(s("t"), 1)

            def weigh(b, a, k):
                pe.wait_ge(s("exp"), b * NH0 + 4 * a + 4)
                if a == 0 and k == 0:
                    pe.wait_ge(s("vp"), b + 1)
                    if b >= 1:
                        pe.wait_ge(s("xm"), b)
                for what in range(2):
                    for j in range(4):
                        h = 4 * a + j
                        lhs = ones_c[:, a, :] if what else vp[b % 2][:, k, h, :]
                        mm = pe.matmul(bank_c[32 * j:32 * j + 32, what * T:(what + 1) * T], lhs,
                                       pt[:, h, k, :], start=(a == 0 and k == 0 and what == 0),
                                       stop=(a == 1 and k == 1), skip_group_check=True)
                mm.then_inc(s("c"), 1)

            def project(b):
                pe.wait_ge(s("cn"), b + 1)
                if b == 0:
                    pe.wait_ge(s_ld["wo"], 16 * NH0)
                pe.matmul(bank_c[:, 0:T], w_o[:, :], cn[:, :], start=True, stop=True).then_inc(s("o"), 1)

            ada_raw = w_raw[1][:, :, :, :].rearrange("p k s n -> p k (s n)")

            def modulation():
                pe.wait_ge(s_ld["small1"], 128)
                pe.wait_ge(s_ld["ada"], 32)
                for i, col in enumerate((0, 1, 2, 3, 6, 7, 8, 9)):
                    for k in range(KT):
                        pe.matmul(bank_s[0][:, i * B:(i + 1) * B], ada_raw[:, k, col * P:(col + 1) * P],
                                  temb_t[:, k, :], start=(k == 0), stop=(k == KT - 1))

            def gate_rows():
                for k in range(KT):
                    mm = pe.matmul(bank_s[1][0:B, :].rearrange("p (g n) -> p g n", g=2), temb_t[:, k, :],
                                   ada_raw[:, k, :].rearrange("p (h g n) -> p h g n", h=2, g=3)[:, :, 2, :],
                                   start=(k == 0), stop=(k == KT - 1))
                mm.then_inc(s("ada"), 1)

            pe.wait_ge(s_ld["wq"], 16)
            pe.wait_ge(s("const"), 5)
            pe.wait_ge(s("wrep"), 3)
            pe.wait_ge(s("rrows"), 2)
            queries(0, 0)
            queries(0, 1)
            modulation()
            gate_rows()
            for b in range(-1, B + 2):
                for h in range(NH0):
                    if 0 <= b < B:
                        if h == 0:
                            pe.wait_ge(s("leftm"), 2 * b + 1)
                        if h == 4:
                            pe.wait_ge(s("leftm"), 2 * b + 2)
                        if b == 0 and h == 0:
                            pe.wait_ge(s("mod"), 1)
                        scores_kq(b, h)
                    if b + 1 < B:
                        if h in (0, 4):
                            pe.wait_ge(s("left"), 2 * (b + 1) + 1 + h // 4)
                            pe.wait_ge(s("right"), 2 * (b + 1) + 1 + h // 4)
                        scores_qk(b + 1, h)
                    if h == 0 and b + 2 < B:
                        queries(b + 2, 0)
                    if h == 3 and b + 2 < B:
                        queries(b + 2, 1)
                    if h == 0 and 0 <= b < B:
                        values(b)
                    if h in (1, 2) and 1 <= b <= B:
                        weigh(b - 1, 1, h - 1)
                    if h == 1 and 0 <= b < B:
                        max_rows(b, 1)
                    if (b, h) in EARLY:
                        what = EARLY[b, h]
                        if what == 0:
                            pe.wait_ge(s("left"), 2 * B)
                            pe.wait_ge(s("zr"), 2 * B)
                            pe.wait_ge(s("xh1"), CH)
                            pe.wait_ge(s("xl1"), CH)
                        if what < CH:
                            project_v(pe, 0, what)
                        else:
                            project_qk(pe, what - CH)
                    if h == 3 and b >= 2:
                        if b < B:
                            pe.wait_ge(s("leftm"), 2 * (b + 1))
                        elif b >= B:
                            pe.wait_ge(s("xf1"), b - 2)
                        ln_transposes(pe, "1", b - 2, bank_m)
                    if h == 5 and 1 <= b <= B:
                        project(b - 1)
                    if h == 5 and b + 1 < B:
                        max_rows(b + 1, 0)
                    if h in (6, 7) and 0 <= b < B:
                        weigh(b, 0, h - 6)

        @blk.scalar
        def _(act):
            act.wait_ge(s_ld["cond"], 32)
            act.activation(c_hi, c_rows, ACT.Copy).then_inc(s("rhi"), 1)
            act.wait_ge(s_ld["small0"], 16)

            def stack(b, n, what):
                two = slice(2 * n, 2 * n + 2)
                if what == 0:
                    act.wait_ge(s("z"), 2 * b + n + 1)
                    if b >= 1:
                        act.wait_ge(s("left"), 2 * b - 1 + n)
                    act.activation(zh[:, two, :].rearrange("p g t -> p (g t)"), bank_z[n][:, :], ACT.Copy)\
                       .then_inc(s("zh"), 1)
                elif what == 1:
                    if b >= 1:
                        act.wait_ge(s("right"), 2 * b - 1 + n)
                    act.activation(zr[:, two, :].rearrange("p g t -> p (g t)"), bank_z[n][:, :], ACT.Identity,
                                   bias=role[:, 3:4], scale=role[:, 2:3])
                else:
                    act.activation(zrh[:, two, :].rearrange("p g t -> p (g t)"), bank_z[n][:, :], ACT.Identity,
                                   bias=role[:, 6:7], scale=role[:, 5:6]).then_inc(s("zr"), 1)

            def value_cols(b):
                act.wait_ge(s("v"), b + 1)
                if b == 0:
                    act.wait_ge(s("vp0"), 2)
                if b >= 2:
                    act.wait_ge(s("c"), 4 * (b - 1))
                v = bank_m[:, 0:2 * P].rearrange("p (k a je) -> p k a je", k=2, a=2)
                for a in range(2):
                    for k in range(2):
                        last = act.activation(vp[b % 2][:, k, 4 * a:4 * a + 4, 16 * a:16 * a + 16],
                                              v[:, k, a, :].rearrange("p (j e) -> p j e", e=DK), ACT.Copy)
                last.then_inc(s("vp"), 1)

            for n in range(2):
                for what in range(3):
                    stack(0, n, what)
            stack_slots = {1: (0, 0), 2: (0, 1), 4: (0, 2), 5: (1, 0), 6: (1, 1), 7: (1, 2)}
            for b in range(-1, B + 2):
                for h in range(NH0):
                    if 0 <= b < B:
                        n = b * NH0 + h
                        act.wait_ge(s("s"), n + 1)
                        if b >= 1 and h % 4 == 0:
                            act.wait_ge(s("c"), 4 * (b - 1) + 2 * (h // 4 + 1))
                        act.activation(pt[:, h, :, :].rearrange("p k t -> p (k t)"), bank_s[n % 2][:, :], ACT.Exp)\
                           .then_inc(s("exp"), 1)
                    if h == 0 and 0 <= b < B:
                        value_cols(b)
                    if h in stack_slots and b + 2 < B:
                        stack(b + 2, *stack_slots[h])
                    if (b, h) in EARLY:
                        what = EARLY[b, h]
                        if what < CH:
                            evacuate_v(act, 0, what)
                        else:
                            evacuate_qk(act, what - CH)
                    if h == 3 and b >= 2:
                        ln_modulate(act, "1", b - 2, bank_m, 0)

        @blk.vector
        def _(dve):
            dve.wait_ge(s("rhi"), 1)
            dve.wait_ge(s_ld["small0"], 16)
            for i in range(2):
                half = slice(i * CH * T, (i + 1) * CH * T)
                dve.scalar_tensor_tensor(out=r_rows[i].rearrange("p b t -> p (b t)"), in0=c_hi[:, half].bitcast(F32),
                                         scalar=role[0:2, 4:5], in1=c_rows[:, half], op0=ALU.mult, op1=ALU.add)\
                   .then_inc(s("rrows"), 1)

            def left_op(b, n):
                dve.wait_ge(s("zr"), 2 * b + n + 1)
                if b >= 2:
                    dve.wait_ge(s("a"), (b - 1) * NH0)
                    dve.wait_ge(s("leftm"), 2 * (b - 1))
                two = slice(2 * n, 2 * n + 2)
                dve.scalar_tensor_tensor(
                    out=left[b % 2][:, two, :].rearrange("p g t -> p (g t)"),
                    in0=zh[:, two, :].rearrange("p g t -> p (g t)").bitcast(F32), scalar=role[:, 0:1],
                    in1=bank_z[n][:, :], op0=ALU.mult, op1=ALU.add).then_inc(s("left"), 1)

            def max_split(b, half):
                n = 2 * b + half
                dve.wait_ge(s("max"), b * NH0 + 4 * half + 4)
                src = nmax[:, 4 * half:4 * half + 4, :]
                hi = nmax_h[:, 4 * half:4 * half + 4, :]
                dve.tensor_copy(hi, src).then_inc(s("nh"), 1)
                dve.wait_ge(s("nh"), n + 1)
                if n == 0:
                    dve.wait_ge(s("mx0"), 1)
                if n >= 2:
                    dve.wait_ge(s("t"), n - 1)
                dst = mx[:, half, :, :, :].rearrange("p k g (i r) -> p g i k r", i=2)
                s4 = src.rearrange("p (g i) k -> p g i k", i=2)
                h4 = hi.rearrange("p (g i) k -> p g i k", i=2).bitcast(F32)
                dve.tensor_copy(dst[:, :, :, :, MAX_ROW], h4)
                dve.tensor_tensor(dst[:, :, :, :, MAX_ROW + 1], s4, h4, ALU.subtract).then_inc(s("mx"), 1)

            def left_with_max(b, half):
                n = 2 * b + half
                dve.wait_ge(s("t"), n + 1)
                if b >= 2:
                    dve.wait_ge(s("s"), (b - 1) * NH0)
                dve.wait_ge(s("left"), 2 * b + 1 + half)
                dve.tensor_tensor(leftm[b % 2][:, 2 * half:2 * half + 2, :].rearrange("p g t -> p (g t)"),
                                  bank_m[:, :],
                                  left[b % 2][:, 2 * half:2 * half + 2, :].rearrange("p g t -> p (g t)").bitcast(F32),
                                  ALU.add).then_inc(s("leftm"), 1)

            def modulation_rows():
                dve.wait_ge(s("ada"), 1)
                dve.tensor_tensor(mod[:, 0:4, :], bank_s[0][:, 0:4 * B].rearrange("p (i b) -> p i b", b=B),
                                  ada_bt[:, 0:4].unsqueeze(2).to_broadcast([P, 4, B]), ALU.add)
                dve.tensor_tensor(mod[:, 4:8, :], bank_s[0][:, 4 * B:8 * B].rearrange("p (i b) -> p i b", b=B),
                                  ada_bt[:, 6:10].unsqueeze(2).to_broadcast([P, 4, B]), ALU.add).then_inc(s("mod0"), 1)
                dve.tensor_tensor(gates[:, :, :], bank_s[1][0:B, :].rearrange("p (g n) -> p g n", g=2), gate_b[:, :, :],
                                  ALU.add)
                dve.tensor_scalar(q_bias[:, :], qkv_bt[:, 0:NH1], SCALE1, None, ALU.mult)
                dve.wait_ge(s("mod0"), 1)
                dve.tensor_scalar(mod[:, :, :].rearrange("p (l i) b -> p l i b", l=2)[:, :, 2:4, :],
                                  mod[:, :, :].rearrange("p (l i) b -> p l i b", l=2)[:, :, 2:4, :],
                                  1.0, None, ALU.add).then_inc(s("mod"), 1)

            def inverse_sums(b, i):
                if i == 0:
                    dve.wait_ge(s("c"), 4 * b + 4)
                dve.reciprocal(dinv[:, i * P:(i + 1) * P], bank_c[:, T + i * P:T + (i + 1) * P]).then_inc(s("dinv"), 1)

            def normalise(b):
                dve.wait_ge(s("dinv"), 2 * b + 2)
                if b >= 1:
                    dve.wait_ge(s("o"), b)
                dve.tensor_tensor(cn[:, :], bank_c[:, 0:T], dinv[:, :], ALU.mult).then_inc(s("cn"), 1)

            for n in range(2):
                left_op(0, n)
            for b in range(-1, B + 2):
                for h in range(NH0):
                    if b + 1 < B:
                        n = (b + 1) * NH0 + h
                        dve.wait_ge(s("a"), n + 1)
                        if h % 4 == 0 and n >= 8:
                            dve.wait_ge(s("mx"), 2 * b + h // 4 + 1)
                        dve.tensor_reduce(nmax[:, h, :], bank_a[n % 2][:, :].rearrange("p (k t) -> p k t", k=2),
                                          AX.X, ALU.max, negate=True).then_inc(s("max"), 1)
                    if h == 0 and b == -1:
                        modulation_rows()
                    if h == 0 and 0 <= b and b + 1 < B:
                        left_op(b + 1, 1)
                    if h == 1 and b >= 2:
                        ln_normal(dve, "1", b - 2, xm)
                    if h == 2 and 0 <= b < B:
                        left_with_max(b, 1)
                    if h == 3 and b + 1 < B:
                        max_split(b + 1, 0)
                    if h in (3, 4) and 1 <= b <= B:
                        inverse_sums(b - 1, h - 3)
                    if h == 4 and 1 <= b <= B:
                        normalise(b - 1)
                    if h == 5 and 1 <= b <= B:
                        dve.wait_ge(s("o"), b)
                        dve.tensor_tensor(xm[:, b - 1, :], bank_c[:, 0:T], x_in[:, b - 1, :], ALU.add)\
                           .then_inc(s("xm"), 1)
                        dve.wait_ge(s("xm"), b)
                        ln_stats(dve, "1", b - 1, xm)
                    if h == 6 and b + 1 < B:
                        left_with_max(b + 1, 0)
                    if h == 6 and b + 2 < B:
                        left_op(b + 2, 0)
                    if h == 7 and b >= 2:
                        ln_low(dve, "1", b - 2)
                    if h == 7 and b + 1 < B:
                        max_split(b + 1, 1)

        l0.close()

        ow_raw = [sb(f"ow_raw{i}", [P, HPG, DIM]) for i in range(2)]
        ow_h = sb("ow_h", [P, NH1, DIM], F32R)
        ow_l = sb("ow_l", [P, NH1, DIM], F32R)
        prob = sb("prob", [P, 2, CH, D])
        prob_t = sb("prob_t", [P, 2, CH, D])
        at_h = sb("at_h", [P, 2, HPG, CT], F32R)
        at_l = sb("at_l", [P, 2, HPG, CT], F32R)
        nm1 = sb("nm1", [P, 2, CH])
        sum1 = sb("sum1", [P, 2, CH])
        rs1 = sb("rs1", [P, 2, CH])

        ctx2 = ExitStack()
        blk = ctx2.enter_context(nc.Block())
        bank_s1 = banks[2:4]
        bank_t1, bank_v1, bank_o1, bank_g = banks[4], banks[5], banks[6], banks[7]
        w1_h = w_qk_h[:, :, :, :].rearrange("p k s n -> p k (s n)")
        w1_l = w_qk_l[:, :, :, :].rearrange("p k s n -> p k (s n)")
        w2_h = w_v_h[:, :, :, :].rearrange("p a k n -> p (a k n)").rearrange("p (m n) -> p m n", m=MB)
        w2_l = w_v_l[:, :, :, :].rearrange("p a k n -> p (a k n)").rearrange("p (m n) -> p m n", m=MB)

        h_h = at_h[:, :, :, :].rearrange("p a j n -> p (a j) n")
        h_l = at_l[:, :, :, :].rearrange("p a j n -> p (a j) n")
        h_f = v_sb[:, :, :, :].rearrange("p a j n -> p (a j) n")

        @blk.sync
        def _(sp):
            def load_ow(g):
                if g >= 2:
                    sp.wait_ge(s("ow"), g - 1)
                sp.dma_start(ow_raw[g % 2][:, :, :],
                             out_w.rearrange("(h p) n -> p h n", p=P)[:, g * HPG:(g + 1) * HPG, :])\
                  .then_inc(s(f"ld_ow{g % 2}"), 16)

            load_ow(0)
            load_ow(1)
            for g in range(2, GROUPS):
                load_ow(g)
                sp.wait_ge(s("wsplit"), 5 * (g - 1))
                load_group(sp, g)
            sp.wait_ge(s("wsplit"), 5 * (GROUPS - 1))
            sp.dma_start(w1_raw, ffn_w1.rearrange("(k p) n -> p k n", p=P)).then_inc(s("ld_w1"), 16)
            sp.wait_ge(s("wsplit"), 5 * GROUPS)
            sp.dma_start(w2_raw, ffn_w2.rearrange("(m p) n -> p m n", p=P)).then_inc(s("ld_w2"), 16)
            for b in range(B):
                sp.wait_ge(s("fin"), b + 1)
                sp.dma_start(out[b], xm[:, b, :]).then_inc(s("out"), 16)
            sp.wait_ge(s("out"), 16 * B)

        MBH = MB // 2
        last_banks = [bank_o1, bank_s1[0], bank_s1[1], bank_v1]

        mb_order = [a * HPG + j for j in range(HPG) for a in range(2)]

        @blk.gpsimd
        def _(pool):
            for g in range(GROUPS):
                hs = slice(g * HPG, (g + 1) * HPG)
                raw = ow_raw[g % 2][:, :, :]
                pool.wait_ge(s(f"ld_ow{g % 2}"), 16 * (g // 2 + 1))
                pool.tensor_copy(ow_h[:, hs, :], raw).then_inc(s("owh"), 1)
                pool.wait_ge(s("owh"), g + 1)
                pool.tensor_tensor(ow_l[:, hs, :], raw, ow_h[:, hs, :].bitcast(F32), ALU.subtract)\
                    .then_inc(s("ow"), 1)
                if g + 1 < GROUPS:
                    split_v(pool, g + 1)
                    for j in range(HPG):
                        split_qk(pool, g + 1, j)
            pool.wait_ge(s("ld_w2"), 16)
            pool.wait_ge(s("p"), proj_no[("v", HGROUPS - 3, CH - 1)] + 1)
            pool.tensor_copy(w2_h[:, 0:MBH, :], w2_raw[:, 0:MBH, :]).then_inc(s("w2h_even"), 1)
            pool.wait_ge(s("w2h_even"), 1)
            pool.tensor_tensor(w2_l[:, 0:MBH, :], w2_raw[:, 0:MBH, :], w2_h[:, 0:MBH, :].bitcast(F32),
                               ALU.subtract).then_inc(s("w2_even"), 1)
            pool.wait_ge(s("ld_w1"), 16)
            def base(b):
                pool.tensor_tensor(xm[:, b, :], xm[:, b, :], acc[:, b, :], ALU.add).then_inc(s("base"), 1)

            for j in range(HPG):
                split_qk(pool, GROUPS, j)
                ln_rstd(pool, "2", j)
                base(j)
            for b in range(CH, B):
                ln_rstd(pool, "2", b)
                base(b)

        @blk.tensor
        def _(pe):
            def scores(n):
                pe.wait_ge(s("pe"), proj_no[("k", n)] + 1)
                if n >= 2:
                    pe.wait_ge(s("exp1"), n - 1)
                for b in range(CH):
                    mm = pe.matmul(bank_s1[n % 2][:, b * D:(b + 1) * D], qk[:, n % 2, 0, b * D:(b + 1) * D],
                                   qk[:, n % 2, 1, b * D:(b + 1) * D], start=True, stop=True)
                mm.then_inc(s("s1"), 1)

            def turn_probs(n):
                pe.wait_ge(s("norm"), n + 1)
                if n >= 1:
                    pe.wait_ge(s("pt1"), n)
                for b in range(CH):
                    mm = pe.transpose(bank_t1[:, b * D:(b + 1) * D], prob[:, n % 2, b, :], ident[:, :])
                mm.then_inc(s("t1"), 1)

            def attend(n):
                m, j, g, c = part(n)
                pe.wait_ge(s("pt1"), n + 1)
                pe.wait_ge(s("pe"), proj_no[("v", m, CH - 1)] + 1)
                if n >= 1:
                    pe.wait_ge(s("atl"), n)
                for b in range(CH):
                    mm = pe.matmul(bank_v1[:, b * D:(b + 1) * D], v_sb[:, m % 2, b, j * DH:(j + 1) * DH],
                                   prob_t[:, n % 2, b, :], start=True, stop=True)
                mm.then_inc(s("av"), 1)

            def out_project(m, k, bank=bank_o1):
                g, c = divmod(m, 2)
                i = m * CH + k
                pe.wait_ge(s("atl"), HPG * (m + 1))
                pe.wait_ge(s("ath"), HPG * (m + 1))
                pe.wait_ge(s("ow"), g + 1)
                if 1 <= i <= CH * (HGROUPS - 1):
                    pe.wait_ge(s("acc"), i)
                cols = slice(k * D, (k + 1) * D)
                for j in range(HPG):
                    mm = three(pe, bank[:, 0:DIM], at_h[:, c, j, cols], at_l[:, c, j, cols],
                               ow_h[:, g * HPG + j, :], ow_l[:, g * HPG + j, :], j == 0, j == HPG - 1)
                mm.then_inc(s("op"), 1)

            def spread_gate(i, which, b):
                if i >= 1:
                    pe.wait_ge(s("gate"), i)
                if 2 <= i < CH:
                    pe.wait_ge(s("xf2"), i - 1)
                pe.matmul(bank_g[:, 0:DIM], sel[:, b, :], gates[:, which, :], start=True, stop=True)\
                    .then_inc(s("g"), 1)

            for n in range(STEPS):
                m, k, g, c = part(n)
                scores(n)
                if n >= 1:
                    attend(n - 1)
                if 1 < n + 1 < STEPS:
                    project_qk(pe, n + 1)
                if n > 0:
                    turn_probs(n)
                if m + 1 < HGROUPS:
                    project_v(pe, m + 1, k)
                if n == 0:
                    turn_probs(n)
                if m == HGROUPS - 1 and k >= 2:
                    pe.wait_ge(s("gate"), k)
                    ln_transposes(pe, "2", k - 2, bank_g)
                if m >= 1:
                    out_project(m - 1, k)
                if m == HGROUPS - 1:
                    spread_gate(k, 0, k)
            attend(STEPS - 1)
            pe.wait_ge(s("pt1"), STEPS)
            ln_transposes(pe, "2", CH - 2, bank_t1)
            for k in range(CH):
                if k == 0:
                    pe.wait_ge(s("acc"), CH * (HGROUPS - 1))
                if k == 1:
                    pe.wait_ge(s("exp1"), STEPS)
                if k == CH - 1:
                    pe.wait_ge(s("atl"), STEPS)
                out_project(HGROUPS - 1, k, last_banks[k])
            pe.wait_ge(s("xf2"), CH - 1)
            ln_transposes(pe, "2", CH - 1, bank_t1)

            for c in range(2):
                for q, mb in enumerate(mb_order):
                    i = c * MB + q
                    if c == 0:
                        pe.wait_ge(s("wsplit"), 5 * GROUPS + 1 + q // 2)
                    if q == 0:
                        pe.wait_ge(s("xh2"), CH * (c + 1))
                        pe.wait_ge(s("xl2"), CH * (c + 1))
                    if c == 0 and q % 2 == 0:
                        spread_gate(CH + q // 2, 0, CH + q // 2)
                    if i < 2:
                        pe.wait_ge(s("pe"), len(order))
                    else:
                        pe.wait_ge(s("gelu"), i - 1)
                    for t in range(KT):
                        cols = slice(mb * P, (mb + 1) * P)
                        mm = three(pe, bank_p[i % 2][:, :], w1_h[:, t, cols], w1_l[:, t, cols],
                                   xh[:, t, c * CT:(c + 1) * CT], xl[:, t, c * CT:(c + 1) * CT],
                                   t == 0, t == KT - 1)
                    mm.then_inc(s("f1"), 1)
                for k in range(CH):
                    b = c * CH + k
                    if b == 0:
                        pe.wait_ge(s("w2_even"), 1)
                        pe.wait_ge(s("w2_odd"), 1)
                        pe.wait_ge(s("acc"), CH * HGROUPS)
                    if b >= 2:
                        pe.wait_ge(s("y"), b - 1)
                    for q, mb in enumerate(mb_order):
                        pe.wait_ge(s("hl"), MB * c + q + 1)
                        cols = slice(k * D, (k + 1) * D)
                        mm = three(pe, bank_s1[b % 2][:, 0:DIM], h_h[:, q, cols], h_l[:, q, cols],
                                   w2_h[:, mb, :], w2_l[:, mb, :], q == 0, q == MB - 1)
                        if q == MBH:
                            spread_gate(B + b, 1, b)
                        if q == MBH and c == 0:
                            pe.wait_ge(s("xf2"), CH + k)
                            ln_transposes(pe, "2", CH + k, bank_t1)
                    mm.then_inc(s("f2"), 1)

        @blk.scalar
        def _(act):
            def attention_high(n):
                m, j, g, c = part(n)
                h = g * HPG + j
                act.wait_ge(s("av"), n + 1)
                if m >= 2:
                    act.wait_ge(s("op"), CH * (m - 1))
                act.activation(at_h[:, c, j, :], bank_v1[:, :], ACT.Identity,
                               bias=qkv_bt[:, 2 * NH1 + h:2 * NH1 + h + 1], scale=1.0).then_inc(s("ath"), 1)

            for n in range(STEPS):
                m, k, g, c = part(n)
                act.wait_ge(s("max1"), n + 1)
                if n >= 2:
                    act.wait_ge(s("t1"), n - 1)
                    act.wait_ge(s("rs1"), n - 1)
                for b in range(CH):
                    last = act.activation(prob[:, n % 2, b, :], bank_s1[n % 2][:, b * D:(b + 1) * D], ACT.Exp,
                                          bias=nm1[:, n % 2, b:b + 1], scale=1.0,
                                          accum_out=sum1[:, n % 2, b:b + 1])
                last.then_inc(s("exp1"), 1)
                if n >= 1:
                    attention_high(n - 1)
                if 1 < n + 1 < STEPS:
                    evacuate_qk(act, n + 1)
                if m + 1 < HGROUPS:
                    evacuate_v(act, m + 1, k)
                if m == HGROUPS - 1 and k >= 2:
                    ln_modulate(act, "2", k - 2, bank_g, 4)
                if n == STEPS - 4:
                    act.wait_ge(s("ld_w2"), 16)
                    act.wait_ge(s("p"), proj_no[("v", HGROUPS - 1, CH - 1)] + 1)
                    act.activation(w2_h[:, MBH:, :], w2_raw[:, MBH:, :], ACT.Copy).then_inc(s("w2h_odd"), 1)
            attention_high(STEPS - 1)
            ln_modulate(act, "2", CH - 2, bank_t1, 4)
            ln_modulate(act, "2", CH - 1, bank_t1, 4)
            for c in range(2):
                for q, mb in enumerate(mb_order):
                    i = c * MB + q
                    act.wait_ge(s("f1"), i + 1)
                    if c == 0:
                        act.wait_ge(s("av"), STEPS - HPG if q < MBH else STEPS)
                        act.wait_ge(s("op"), CH * (HGROUPS - 1) if q < MBH else CH * HGROUPS)
                    else:
                        act.wait_ge(s("hl"), q + 1)
                    act.activation(h_f[:, q, :], bank_p[i % 2][:, :], ACT.Gelu, bias=b1_t[:, mb:mb + 1], scale=1.0)\
                       .then_inc(s("gelu"), 1)
                    act.wait_ge(s("gelu"), i + 1)
                    if c == 1:
                        act.wait_ge(s("f2"), CH)
                    act.activation(h_h[:, q, :], h_f[:, q, :], ACT.Copy).then_inc(s("hh"), 1)
                for k in range(CH if c == 0 else 0):
                    ln_modulate(act, "2", CH + k, bank_t1, 4)

        @blk.vector
        def _(dve):
            def attention_low(n):
                m, j, g, c = part(n)
                h = g * HPG + j
                dve.wait_ge(s("ath"), n + 1)
                dve.scalar_tensor_tensor(out=at_l[:, c, j, :], in0=bank_v1[:, :],
                                         scalar=qkv_bt[:, 2 * NH1 + h:2 * NH1 + h + 1],
                                         in1=at_h[:, c, j, :].bitcast(F32), op0=ALU.add, op1=ALU.subtract)\
                   .then_inc(s("atl"), 1)

            def accumulate(m, k, bank=bank_o1):
                g, c = divmod(m, 2)
                b = c * CH + k
                dve.wait_ge(s("op"), m * CH + k + 1)
                if g >= 1:
                    dve.wait_ge(s("acc"), (m - 2) * CH + k + 1)
                dve.tensor_tensor(acc[:, b, :], bank[:, 0:DIM], out_b_bc[:, :] if g == 0 else acc[:, b, :],
                                  ALU.add).then_inc(s("acc"), 1)

            def add_gated(b):
                dve.wait_ge(s("g"), b + 1)
                dve.wait_ge(s("acc"), (HGROUPS - 2) * CH + b + 1)
                dve.tensor_tensor(acc[:, b, :], acc[:, b, :], bank_g[:, 0:DIM], ALU.mult).then_inc(s("gate"), 1)

            def residual(b):
                dve.wait_ge(s("gate"), b + 1)
                dve.tensor_tensor(acc[:, b, :], acc[:, b, :], xm[:, b, :], ALU.add).then_inc(s("res"), 1)
                dve.wait_ge(s("res"), b + 1)
                ln_stats(dve, "2", b, acc)

            for n in range(STEPS):
                m, k, g, c = part(n)
                dve.wait_ge(s("s1"), n + 1)
                dve.tensor_reduce(nm1[:, n % 2, :], bank_s1[n % 2][:, :].rearrange("p (b t) -> p b t", b=CH),
                                  AX.X, ALU.max, negate=True).then_inc(s("max1"), 1)
                dve.wait_ge(s("exp1"), n + 1)
                dve.reciprocal(rs1[:, n % 2, :], sum1[:, n % 2, :]).then_inc(s("rs1"), 1)
                dve.wait_ge(s("rs1"), n + 1)
                dve.tensor_tensor(prob[:, n % 2, :, :], prob[:, n % 2, :, :],
                                  rs1[:, n % 2, :].unsqueeze(2).to_broadcast([P, CH, D]), ALU.mult)\
                   .then_inc(s("norm"), 1)
                if m == HGROUPS - 1 and k >= 2:
                    ln_normal(dve, "2", k - 2, acc)
                if n >= 1:
                    attention_low(n - 1)
                if n > HPG:
                    accumulate(*divmod(n - 1 - HPG, HPG))
                if m == HGROUPS - 1 and k >= 1:
                    add_gated(k - 1)
                dve.wait_ge(s("t1"), n + 1)
                if n >= 2:
                    dve.wait_ge(s("av"), n - 1)
                dve.tensor_copy(prob_t[:, n % 2, :, :].rearrange("p b t -> p (b t)"), bank_t1[:, :])\
                   .then_inc(s("pt1"), 1)
                if m == HGROUPS - 1 and k >= 1:
                    residual(k - 1)
                if m == HGROUPS - 1 and k >= 2:
                    ln_low(dve, "2", k - 2)
                if n == STEPS - 3:
                    dve.wait_ge(s("w2h_odd"), 1)
                    dve.tensor_tensor(w2_l[:, MBH:, :], w2_raw[:, MBH:, :], w2_h[:, MBH:, :].bitcast(F32),
                                      ALU.subtract).then_inc(s("w2_odd"), 1)
            accumulate(HGROUPS - 2, CH - 1)
            add_gated(CH - 1)
            ln_normal(dve, "2", CH - 2, acc)
            residual(CH - 1)
            attention_low(STEPS - 1)
            ln_low(dve, "2", CH - 2)
            ln_normal(dve, "2", CH - 1, acc)
            for k in range(CH):
                accumulate(HGROUPS - 1, k, last_banks[k])
            ln_low(dve, "2", CH - 1)
            for c in range(2):
                for q in range(MB):
                    i = c * MB + q
                    if c == 0 and q % 2 == 0:
                        add_gated(CH + q // 2)
                    dve.wait_ge(s("hh"), i + 1)
                    dve.tensor_tensor(h_l[:, q, :], h_f[:, q, :], h_h[:, q, :].bitcast(F32), ALU.subtract)\
                       .then_inc(s("hl"), 1)
                    if c == 0 and q % 2 == 1:
                        residual(CH + q // 2)
                for k in range(CH):
                    b = c * CH + k
                    if c == 0:
                        if k == 0:
                            ln_normal(dve, "2", CH, acc)
                        if k + 1 < CH:
                            ln_normal(dve, "2", CH + k + 1, acc)
                        ln_low(dve, "2", CH + k)
                    dve.wait_ge(s("f2"), b + 1)
                    dve.wait_ge(s("base"), b + 1)
                    dve.tensor_tensor(acc[:, b, :], bank_s1[b % 2][:, 0:DIM], b2_bc[:, :], ALU.add).then_inc(s("y"), 1)
                    dve.wait_ge(s("y"), b + 1)
                    dve.wait_ge(s("g"), B + b + 1)
                    dve.tensor_tensor(acc[:, b, :], acc[:, b, :], bank_g[:, 0:DIM], ALU.mult)\
                       .then_inc(s("gate"), 1)
                    dve.wait_ge(s("gate"), B + b + 1)
                    dve.tensor_tensor(xm[:, b, :], xm[:, b, :], acc[:, b, :], ALU.add).then_inc(s("fin"), 1)

        ctx2.close()


_INPUTS = ["x", "cond", "cond_t", "wq_t", "wo_t", "ada_w", "ada_b", "ada_b_t", "qkv_w", "qkv_b_t", "out_w", "out_b",
           "ffn_w1", "ffn_b1_t", "ffn_w2", "ffn_b2", "roles"]


def lay_out(inputs):
    import numpy as np
    c = np.ascontiguousarray
    i = {k: np.asarray(v) for k, v in inputs.items()}
    return {
        "x": i["x"], "cond": i["cond_2048"], "cond_t": c(i["cond_2048"].T),
        "wq_t": c(i["L0_cond_Wq"].T), "wo_t": c(i["L0_cond_Wo"].T),
        "ada_w": i["L1_cond_ada_w"], "ada_b": i["L1_cond_ada_b"],
        "ada_b_t": c(i["L1_cond_ada_b"].reshape(12, P).T),
        "qkv_w": i["L1_cond_qkv_w"], "qkv_b_t": c(i["L1_cond_qkv_b"].reshape(3 * NH1, DH).T),
        "out_w": i["L1_cond_out_w"], "out_b": i["L1_cond_out_b"],
        "ffn_w1": i["L1_cond_ffn_w1"], "ffn_b1_t": c(i["L1_cond_ffn_b1"].reshape(MB, P).T),
        "ffn_w2": i["L1_cond_ffn_w2"], "ffn_b2": i["L1_cond_ffn_b2"], "roles": row_roles(),
    }


def kernel(**inputs):
    import numpy as np
    import concourse.bacc as bacc
    from concourse.bass_utils import run_bass_kernel_spmd

    nc = bacc.Bacc("TRN2", target_bir_lowering=False, num_devices=1)
    arrays = lay_out(inputs)
    aps = {n: nc.dram_tensor(n + "_dram", a.shape, mybir.dt.from_np(a.dtype), kind="ExternalInput").ap()
           for n, a in arrays.items()}
    aps["out"] = nc.dram_tensor("out_dram", (B, D, DIM), F32, kind="ExternalOutput").ap()
    build_program(nc, **aps)
    result = run_bass_kernel_spmd(nc, [{n + "_dram": a for n, a in arrays.items()}], core_ids=[0])
    return result.results[0]["out_dram"]
```

```python
from contextlib import ExitStack

import concourse.bass as bass
from concourse import mybir

F32 = mybir.dt.float32
F32R = mybir.dt.float32r
ALU = mybir.AluOpType
ACT = mybir.ActivationFunctionType
AX = mybir.AxisListType

P = 128
B = 8
T = 256
D = 128
NH0, DK = 8, 16
NH1, DH = 16, 128
DIM, INNER, MLP = T, NH1 * DH, 4 * T
KT = DIM // P
NEG = 1e30
LN_EPS = 1e-6
SCALE1 = float(DH) ** -0.5

HEAD_ROWS = 64
MASK_ROW = 3 * DK
MAX_ROW = MASK_ROW + 3
PAIRS = NH0 // 2
RING = NH0 + 6
HPG = 4
GROUPS = NH1 // HPG
CH = B // 2
CT = CH * D
STEPS = GROUPS * 2 * HPG
MB = MLP // P
WARM_UPS = 3
MASK_PARTS = ((0, 1), (1, CH), (CH, B))
EARLY = {(6, 0): 0, (6, 2): 1, (7, 0): 2, (7, 2): 3, (8, 7): 4, (9, 4): 5}


def row_roles():
    import numpy as np
    t = np.zeros((P, 7), np.float32)
    t[1, 4] = -1.0
    for i in range(2):
        o = i * HEAD_ROWS
        t[o:o + 3 * DK, 2] = 0.25
        t[o + DK:o + 2 * DK, 1] = -1.0
        t[o + 2 * DK:o + 3 * DK, 0] = -1.0
        t[o + MASK_ROW:o + MASK_ROW + 3, 2] = NEG
        t[o + MASK_ROW:o + MASK_ROW + 3, 3] = -NEG
        t[o + MASK_ROW + 1, 1] = -1.0
        t[o + MASK_ROW + 2, 0] = -1.0
        t[o + MAX_ROW:o + MAX_ROW + 2, 3] = 1.0
    t[:, 5:7] = t[:, 1:2] * t[:, 2:4]
    return t


def build_program(nc, x, cond, cond_t, wq_t, wo_t, ada_w, ada_b, ada_b_t, qkv_w, qkv_b_t, out_w, out_b,
                  ffn_w1, ffn_b1_t, ffn_w2, ffn_b2, roles, out):
    ctx = ExitStack()
    with ctx:
        def sb(name, shape, dt=F32):
            return ctx.enter_context(nc.sbuf_tensor(name, shape, dt))

        def sem(name):
            return ctx.enter_context(nc.semaphore(name))

        ident = sb("ident", [P, P])
        role = sb("role", [P, 7])
        temb_t = sb("temb_t", [P, KT, B])
        ada_bt = sb("ada_bt", [P, 12])
        gate_b = sb("gate_b", [B, 2, DIM])
        qkv_bt = sb("qkv_bt", [P, 3 * NH1])
        q_bias = sb("q_bias", [P, NH1])
        b1_t = sb("b1_t", [P, MB])
        out_b_bc = sb("out_b_bc", [P, DIM])
        b2_bc = sb("b2_bc", [P, DIM])
        mod = sb("mod", [P, 8, B])
        gates = sb("gates", [B, 2, DIM])
        sel = sb("sel", [B, B, P])
        pw = sb("pw", [P, B])
        stats = sb("stats", [P, B, 6])
        mv = sb("mv", [P, B, 2])
        veps = sb("veps", [P, B])
        rstd = sb("rstd", [P, B])
        xm = sb("xm", [P, B, DIM])
        acc = sb("acc", [P, B, DIM])
        xh = sb("xh", [P, KT, B * D], F32R)
        xl = sb("xl", [P, KT, B * D], F32R)
        xn = sb("xn", [P, 2, DIM])
        xn_f = sb("xn_f", [P, 2, KT, D])
        v_sb = sb("v_sb", [P, 2, CH, HPG * DH])
        qk = sb("qk", [P, 2, 2, CT])
        w_raw = [sb(f"w_raw{i}", [P, KT, 3, HPG * DH]) for i in range(2)]
        w_qk_h = sb("w_qk_h", [P, KT, 2, HPG * DH], F32R)
        w_qk_l = sb("w_qk_l", [P, KT, 2, HPG * DH], F32R)
        w_v_h = sb("w_v_h", [P, 2, KT, HPG * DH], F32R)
        w_v_l = sb("w_v_l", [P, 2, KT, HPG * DH], F32R)

        banks = [ctx.enter_context(nc.psum_tensor(f"bank{i}", [P, 512], F32)) for i in range(8)]
        s_xin = [sem(f"s_xin{b}") for b in range(B)]
        s_ld = {k: sem("s_ld_" + k) for k in ("small0", "cond", "wq", "wo", "small1", "ada")}
        s_wraw = [sem(f"s_wraw{i}") for i in range(2)]
        S = {}

        def s(name):
            if name not in S:
                S[name] = sem("s_" + name)
            return S[name]

        def three(pe, dst, ah, al, bh, bl, start, stop):
            pe.matmul(dst, al, bh, start=start, stop=False)
            pe.matmul(dst, ah, bl, start=False, stop=False)
            return pe.matmul(dst, ah, bh, start=False, stop=stop)

        def ln_stats(dve, name, b, src):
            dve.bn_stats(stats[:, b, :], src[:, b, :]).then_inc(s("ln_sums" + name), 1)
            dve.wait_ge(s("ln_sums" + name), b + 1)
            dve.bn_aggr(mv[:, b, :], stats[:, b, :]).then_inc(s("ln_moments" + name), 1)

        def ln_rstd(pool, name, b):
            pool.wait_ge(s("ln_moments" + name), b + 1)
            pool.tensor_scalar(veps[:, b:b + 1], mv[:, b, 1:2], LN_EPS, None, ALU.add).then_inc(s("ln_eps" + name), 1)
            pool.wait_ge(s("ln_eps" + name), b + 1)
            pool.tensor_tensor(rstd[:, b:b + 1], veps[:, b:b + 1], pw[:, b:b + 1], ALU.pow)\
                .then_inc(s("ln_rstd" + name), 1)

        def ln_normal(dve, name, b, src):
            dve.wait_ge(s("ln_rstd" + name), b + 1)
            if b >= 2:
                dve.wait_ge(s("ln_turned" + name), b - 1)
            dve.tensor_scalar(xn[:, b % 2, :], src[:, b, :], mv[:, b, 0:1], rstd[:, b:b + 1],
                              ALU.subtract, ALU.mult).then_inc(s("ln_normal" + name), 1)

        def ln_transposes(pe, name, b, bank):
            pe.wait_ge(s("ln_normal" + name), b + 1)
            for k in range(KT):
                mm = pe.transpose(bank[:, k * P:(k + 1) * P], xn[:, b % 2, k * P:(k + 1) * P], ident[:, :])
            mm.then_inc(s("ln_turned" + name), 1)

        def ln_modulate(act, name, b, bank, shift):
            act.wait_ge(s("ln_turned" + name), b + 1)
            if b == 0:
                act.wait_ge(s("modulation"), 1)
            if b >= 2:
                act.wait_ge(s("ln_low" + name), b - 1)
            for k in range(KT):
                last = act.activation(xn_f[:, b % 2, k, :], bank[:, k * P:(k + 1) * P], ACT.Identity,
                                      bias=mod[:, shift + k, b:b + 1], scale=mod[:, shift + 2 + k, b:b + 1])
            last.then_inc(s("ln_modulated" + name), 1)
            act.wait_ge(s("ln_modulated" + name), b + 1)
            act.activation(xh[:, :, b * D:(b + 1) * D], xn_f[:, b % 2, :, :], ACT.Copy).then_inc(s("ln_high" + name), 1)

        def ln_low(dve, name, b):
            dve.wait_ge(s("ln_high" + name), b + 1)
            dve.tensor_tensor(xl[:, :, b * D:(b + 1) * D], xn_f[:, b % 2, :, :],
                              xh[:, :, b * D:(b + 1) * D].bitcast(F32), ALU.subtract).then_inc(s("ln_low" + name), 1)

        def heads_cols(t, j):
            return t[:, :, 0:2, j * DH:(j + 1) * DH]

        HGROUPS = 2 * GROUPS

        def part(n):
            m, k = divmod(n, HPG)
            return m, k, m // 2, m % 2

        proj_no = {}
        order = [("v", 0, k) for k in range(CH)] + [("q", 0), ("k", 0)]
        for n in range(STEPS):
            m, k, hg, c = part(n)
            if n + 1 < STEPS:
                order += [("q", n + 1), ("k", n + 1)]
            if m + 1 < HGROUPS:
                order += [("v", m + 1, k)]
        for i, what in enumerate(order):
            proj_no[what] = i

        w1_raw = w_raw[0][:, :, :, :].rearrange("p k s n -> p (k s n)")[:, 0:KT * MLP]\
            .rearrange("p (k n) -> p k n", k=KT)
        w2_raw = w_raw[1][:, :, :, :].rearrange("p k s n -> p (k s n)")[:, 0:MB * DIM]\
            .rearrange("p (m n) -> p m n", m=MB)

        def split_v(pool, g):
            pool.wait_ge(s_wraw[g % 2], 32 * (g // 2 + 1))
            if g >= 2:
                pool.wait_ge(s("projections"), proj_no[("v", 2 * (g - 2) + 1, CH - 1)] + 1)
            src = w_raw[g % 2][:, :, 2, :]
            pool.tensor_copy(w_v_h[:, g % 2, :, :], src).then_inc(s("weights_high"), 1)
            pool.wait_ge(s("weights_high"), 5 * g + 1)
            pool.tensor_tensor(w_v_l[:, g % 2, :, :], src, w_v_h[:, g % 2, :, :].bitcast(F32), ALU.subtract)\
                .then_inc(s("weights_split"), 1)

        def split_qk(pool, g, j):
            if g >= 1:
                pool.wait_ge(s("projections"), proj_no[("k", (2 * (g - 1) + 1) * HPG + j)] + 1)
            if g < GROUPS:
                src = heads_cols(w_raw[g % 2], j)
            else:
                src = heads_cols(w1_raw.rearrange("p k (s n) -> p k s n", s=2), j)
            for k in range(KT):
                last = pool.tensor_copy(heads_cols(w_qk_h, j)[:, k, :, :], src[:, k, :, :])
            last.then_inc(s("weights_high"), 1)
            before = 5 * g + 1 if g < GROUPS else 5 * GROUPS
            pool.wait_ge(s("weights_high"), before + 1 + j)
            for k in range(KT):
                last = pool.tensor_tensor(heads_cols(w_qk_l, j)[:, k, :, :], src[:, k, :, :],
                                          heads_cols(w_qk_h, j)[:, k, :, :].bitcast(F32), ALU.subtract)
            last.then_inc(s("weights_split"), 1)

        def load_group(sp, g):
            for k in range(KT):
                sp.dma_start(w_raw[g % 2][:, k, :, :],
                             qkv_w[k * P:(k + 1) * P, :].rearrange("p (s n) -> p s n", s=3)
                             [:, :, g * HPG * DH:(g + 1) * HPG * DH]).then_inc(s_wraw[g % 2], 16)

        bank_p = banks[0:2]

        def take_bank(pe, i):
            if i >= 2:
                pe.wait_ge(s("projections_read"), i - 1)

        def project_v(pe, m, k):
            i = proj_no[("v", m, k)]
            take_bank(pe, i)
            g, c = divmod(m, 2)
            b = c * CH + k
            if k == 0 and c == 0:
                pe.wait_ge(s("weights_split"), 5 * g + 1)
            for t in range(KT):
                mm = three(pe, bank_p[i % 2][:, :], xh[:, t, b * D:(b + 1) * D], xl[:, t, b * D:(b + 1) * D],
                           w_v_h[:, g % 2, t, :], w_v_l[:, g % 2, t, :], t == 0, t == KT - 1)
            mm.then_inc(s("projections"), 1)

        def project_qk(pe, n):
            m, j, g, c = part(n)
            if c == 0:
                pe.wait_ge(s("weights_split"), 5 * g + 2 + j)
            for w, name in enumerate("qk"):
                i = proj_no[(name, n)]
                take_bank(pe, i)
                for t in range(KT):
                    cols = slice(j * DH, (j + 1) * DH)
                    mm = three(pe, bank_p[i % 2][:, :], w_qk_h[:, t, w, cols], w_qk_l[:, t, w, cols],
                               xh[:, t, c * CT:(c + 1) * CT], xl[:, t, c * CT:(c + 1) * CT],
                               t == 0, t == KT - 1)
                mm.then_inc(s("projections"), 1)

        def evacuate_v(act, m, k):
            i = proj_no[("v", m, k)]
            act.wait_ge(s("projections"), i + 1)
            if m >= 2:
                act.wait_ge(s("attention"), HPG * (m - 1))
            act.activation(v_sb[:, m % 2, k, :], bank_p[i % 2][:, :], ACT.Copy).then_inc(s("projections_read"), 1)

        def evacuate_qk(act, n):
            m, j, g, c = part(n)
            for w, name in enumerate("qk"):
                i = proj_no[(name, n)]
                act.wait_ge(s("projections"), i + 1)
                if n >= 2:
                    act.wait_ge(s("scores"), n - 1)
                h = g * HPG + j
                bias = q_bias[:, h:h + 1] if w == 0 else qkv_bt[:, NH1 + h:NH1 + h + 1]
                act.activation(qk[:, n % 2, w, :], bank_p[i % 2][:, :], ACT.Identity, bias=bias,
                               scale=SCALE1 if w == 0 else 1.0).then_inc(s("projections_read"), 1)

        l0 = ExitStack()

        def sb0(name, shape, dt=F32):
            return l0.enter_context(nc.sbuf_tensor(name, shape, dt))

        rbc = sb0("rbc", [P, B, T])
        c_hi = xh[0:2, :, :].rearrange("p k (b t) -> p (k b) t", t=T)
        r_rows = [t[0:2, 1, :, :].rearrange("p k (b t) -> p (k b) t", t=T) for t in (w_v_h, w_v_l)]
        e_rows = sb0("e_rows", [2, P], F32R)
        w_q = sb0("w_q", [P, P])
        w_rep = sb0("w_rep", [P, PAIRS, P])
        w_o = sb0("w_o", [P, P])
        ones_c = sb0("ones_c", [P, 2, 32])
        zr = acc[:, 0:PAIRS, :]
        xr = [acc[:, PAIRS + i, :] for i in range(2)]
        dinv, cn = acc[:, PAIRS + 2, :], acc[:, PAIRS + 3, :]
        zh = sb0("zh", [P, PAIRS, T], F32R)
        zrh = sb0("zrh", [P, PAIRS, T], F32R)
        left = [sb0(f"left{i}", [P, PAIRS, T], F32R) for i in range(2)]
        leftm = sb0("leftm", [P, PAIRS, T], F32R)
        right = [sb0(f"right{i}", [P, PAIRS, T], F32R) for i in range(3)]
        nmax = sb0("nmax", [P, NH0, 2])
        nmax_h = sb0("nmax_h", [P, NH0, 2], F32R)
        mx = sb0("mx", [P, 2, 2, 2, P])
        pt = sb0("pt", [P, RING, 2, T])
        vp = [sb0(f"vp{i}", [P, 2, NH0, 32]) for i in range(2)]

        bank_z = banks[0:2]
        bank_a, bank_s = banks[2:4], banks[4:6]
        bank_c, bank_m = banks[6], banks[7]

        blk = l0.enter_context(nc.Block())

        @blk.sync
        def _(sp):
            sp.dma_start(w_q[:, :], wq_t).then_inc(s_ld["wq"], 16)
            sp.dma_start(rbc[:, :, :], cond.partition_broadcast(P)).then_inc(s_ld["cond"], 16)
            for b in range(B):
                sp.dma_start(xm[:, b, :], x[b]).then_inc(s_xin[b], 16)
                if b == 0:
                    sp.dma_start(role[:, :], roles).then_inc(s_ld["small0"], 16)
                if b == 1:
                    sp.dma_start(temb_t[:, :, :], cond_t.rearrange("(k p) b -> p k b", p=P)).then_inc(s_ld["small1"], 16)
                    sp.dma_start(ada_bt[:, :], ada_b_t).then_inc(s_ld["small1"], 16)
                    for g in range(2):
                        sp.dma_start(gate_b[:, g, :], ada_b[(3 * g + 2) * DIM:(3 * g + 3) * DIM].partition_broadcast(B))\
                          .then_inc(s_ld["small1"], 16)
                    sp.dma_start(qkv_bt[:, :], qkv_b_t).then_inc(s_ld["small1"], 16)
                    sp.dma_start(b1_t[:, :], ffn_b1_t).then_inc(s_ld["small1"], 16)
                    sp.dma_start(out_b_bc[:, :], out_b.partition_broadcast(P)).then_inc(s_ld["small1"], 16)
                    sp.dma_start(b2_bc[:, :], ffn_b2.partition_broadcast(P)).then_inc(s_ld["small1"], 16)
                    for k in range(KT):
                        sp.dma_start(w_raw[1][:, k, :, :].rearrange("p s n -> p (s n)"), ada_w[k * P:(k + 1) * P, :])\
                          .then_inc(s_ld["ada"], 16)
            for h in range(NH0):
                r = 32 * (h % 4) + 16 * (h // 4)
                sp.dma_start(w_o[r:r + DK, :], wo_t[h * DK:(h + 1) * DK, :]).then_inc(s_ld["wo"], 16)
            load_group(sp, 0)
            sp.wait_ge(s("shift_scale_products"), 8)
            load_group(sp, 1)

        @blk.gpsimd
        def _(pool):
            pool.memset(mx[:, :, :, :, :], 0.0).then_inc(s("max_columns_zeroed"), 1)
            pool.memset(w_rep[:, :, :], 0.0).then_inc(s("zeroed"), 1)
            pool.memset(e_rows[:, :].bitcast(F32), 0.0).then_inc(s("zeroed"), 1)
            pool.memset(ident[:, :], 0.0).then_inc(s("zeroed"), 1)
            pool.memset(ones_c[:, :, :], 0.0).then_inc(s("zeroed"), 1)
            for i in range(2):
                pool.memset(vp[i][:, :, :, :], 0.0).then_inc(s("value_columns_zeroed"), 1)
            pool.memset(sel[:, :, :], 0.0).then_inc(s("zeroed"), 1)
            pool.memset(pw[:, :], -0.5).then_inc(s("exponent"), 1)
            pool.wait_ge(s("zeroed"), 5)
            pool.memset(e_rows[:, :].bitcast(F32).rearrange("p (i r) -> p i r", i=2)[:, :, MASK_ROW:MASK_ROW + 3], 1.0)\
                .then_inc(s("constants"), 1)
            for a in range(2):
                pool.memset(ones_c[:, a, 16 * a:16 * a + 16], 1.0).then_inc(s("constants"), 1)
            pool.affine_select(out=ident[:, :], in_=ident[:, :], compare_op=ALU.not_equal, fill=1.0, base=0,
                               pattern=[[-1, P]], channel_multiplier=1).then_inc(s("constants"), 1)
            pool.affine_select(out=sel[:, :, :], in_=sel[:, :, :], compare_op=ALU.not_equal, fill=1.0, base=0,
                               pattern=[[-1, B], [0, P]], channel_multiplier=1).then_inc(s("constants"), 1)
            pool.wait_ge(s_ld["wq"], 16)
            for k in range(3):
                pool.tensor_copy(w_rep[:, :, :].rearrange("p g (i r) -> p (g i) r", i=2)[:, :, k * DK:(k + 1) * DK],
                                 w_q[:, :].rearrange("p (h e) -> p h e", e=DK)).then_inc(s("query_weights"), 1)

            def masked_x(b):
                pool.wait_ge(s_xin[b], 16)
                if b == 0:
                    pool.wait_ge(s_ld["cond"], 16)
                if b >= 2:
                    pool.wait_ge(s("queries"), 2 * (b - 1))
                pool.tensor_tensor(xr[b % 2][:, :], xm[:, b, :], rbc[:, b, :], ALU.mult).then_inc(s("masked_x"), 1)

            def right_op(b, n):
                pool.wait_ge(s("right_parts"), 2 * b + n + 1)
                if b >= 3:
                    pool.wait_ge(s("scores_k"), (b - 2) * NH0)
                two = slice(2 * n, 2 * n + 2)
                pool.tensor_tensor(right[b % 3][:, two, :], zr[:, two, :], zrh[:, two, :].bitcast(F32), ALU.add)\
                    .then_inc(s("right"), 1)

            pool.wait_ge(s_ld["small0"], 16)
            for b in range(2):
                masked_x(b)
            for b in range(2):
                right_op(0, b)
            for b in range(-1, B + 3):
                if b + 3 < B:
                    masked_x(b + 3)
                if b + 2 < B:
                    right_op(b + 2, 0)
                if 2 <= b <= B + 1:
                    ln_rstd(pool, "1", b - 2)
                if b >= 3:
                    ln_low(pool, "1", b - 3)
                if b == 0:
                    split_v(pool, 0)
                if 1 <= b <= HPG:
                    split_qk(pool, 0, b - 1)
                if b + 2 < B:
                    right_op(b + 2, 1)

        @blk.tensor
        def _(pe):
            def queries(b, n):
                pe.wait_ge(s("masked_x"), b + 1)
                pe.wait_ge(s("mask_rows"), 1 if b == 0 else 2 if b < CH else 3)
                if b >= 1:
                    pe.wait_ge(s("left"), 2 * b - 1 + n)
                    pe.wait_ge(s("right_parts"), 2 * b - 1 + n)
                pe.matmul(bank_z[n][:, :], e_rows[:, :],
                          r_rows[b // CH][:, b % CH, :].unsqueeze(1).to_broadcast([2, 2, T]), start=True, stop=False)
                for i in range(2):
                    mm = pe.matmul(bank_z[n][:, i * T:(i + 1) * T], w_rep[:, 2 * n + i, :], xr[b % 2][:, :],
                                   start=False, stop=(i == 1))
                mm.then_inc(s("queries"), 1)

            def values(b):
                pe.wait_ge(s_xin[b], 16)
                pe.wait_ge(s("left_with_max"), 2 * b + 1)
                for k in range(2):
                    mm = pe.matmul(bank_m[:, k * P:(k + 1) * P], xm[:, b, k * P:(k + 1) * P], w_q[:, :],
                                   start=True, stop=True)
                mm.then_inc(s("values"), 1)

            def scores_qk(b, h):
                n = b * NH0 + h
                if n >= 2:
                    pe.wait_ge(s("row_max"), n - 1)
                g, o = h // 2, HEAD_ROWS * (h % 2)
                for k in range(2):
                    mm = pe.matmul(bank_a[n % 2][:, k * T:(k + 1) * T],
                                   left[b % 2][o:o + MAX_ROW, g, k * P:(k + 1) * P],
                                   right[b % 3][o:o + MAX_ROW, g, :], start=True, stop=True)
                mm.then_inc(s("scores_q"), 1)

            def scores_kq(b, h):
                n = b * NH0 + h
                if n >= 2:
                    pe.wait_ge(s("exps"), n - 1)
                g, o = h // 2, HEAD_ROWS * (h % 2)
                for k in range(2):
                    mm = pe.matmul(bank_s[n % 2][:, k * T:(k + 1) * T],
                                   right[b % 3][o:o + MAX_ROW + 2, g, k * P:(k + 1) * P],
                                   leftm[o:o + MAX_ROW + 2, g, :], start=True, stop=True)
                mm.then_inc(s("scores_k"), 1)

            def max_rows(b, half):
                n = 2 * b + half
                pe.wait_ge(s("max_columns"), n + 1)
                if half == 0:
                    if b >= 1:
                        pe.wait_ge(s("left_with_max"), n)
                    if b >= 4:
                        pe.wait_ge(s("ln_modulated1"), b - 3)
                else:
                    pe.wait_ge(s("value_columns"), b + 1)
                for g in range(2):
                    for k in range(2):
                        mm = pe.transpose(bank_m[:, (2 * g + k) * P:(2 * g + k + 1) * P],
                                          mx[:, half, k, g, :], ident[:, :])
                mm.then_inc(s("max_rows"), 1)

            def weigh(b, a, k):
                pe.wait_ge(s("exps"), b * NH0 + 4 * a + 4)
                if a == 0 and k == 0:
                    pe.wait_ge(s("value_columns"), b + 1)
                    if b == 0:
                        pe.wait_ge(s("modulation"), 1)
                    else:
                        pe.wait_ge(s("layer0_out"), b)
                for what in range(2):
                    for j in range(4):
                        h = 4 * a + j
                        lhs = ones_c[:, a, :] if what else vp[b % 2][:, k, h, :]
                        mm = pe.matmul(bank_c[32 * j:32 * j + 32, what * T:(what + 1) * T], lhs,
                                       pt[:, (b * NH0 + h) % RING, k, :], start=(a == 0 and k == 0 and what == 0),
                                       stop=(a == 1 and k == 1), skip_group_check=True)
                mm.then_inc(s("weighed"), 1)

            def project(b):
                pe.wait_ge(s("normalised"), b + 1)
                if b == 0:
                    pe.wait_ge(s_ld["wo"], 16 * NH0)
                pe.matmul(bank_c[:, 0:T], w_o[:, :], cn[:, :], start=True, stop=True).then_inc(s("projected"), 1)

            ada_raw = w_raw[1][:, :, :, :].rearrange("p k s n -> p k (s n)")

            def modulation(i):
                if i == 0:
                    pe.wait_ge(s_ld["small1"], 128)
                    pe.wait_ge(s_ld["ada"], 32)
                col = (0, 1, 2, 3, 6, 7, 8, 9)[i]
                for k in range(KT):
                    mm = pe.matmul(bank_c[:, i * B:(i + 1) * B], ada_raw[:, k, col * P:(col + 1) * P],
                                   temb_t[:, k, :], start=(k == 0), stop=(k == KT - 1))
                mm.then_inc(s("shift_scale_products"), 1)

            def gate_rows():
                for k in range(KT):
                    mm = pe.matmul(bank_s[1][0:B, :].rearrange("p (g n) -> p g n", g=2), temb_t[:, k, :],
                                   ada_raw[:, k, :].rearrange("p (h g n) -> p h g n", h=2, g=3)[:, :, 2, :],
                                   start=(k == 0), stop=(k == KT - 1))
                mm.then_inc(s("gate_products"), 1)

            pe.wait_ge(s("max_columns_zeroed"), 1)
            for i in range(WARM_UPS):
                pe.matmul(bank_m[:, :], mx[:, 0, 0, 0, :], mx[:, 0, :, :, :].rearrange("p k g r -> p (k g r)"),
                          start=True, stop=True)
            pe.wait_ge(s_ld["wq"], 16)
            pe.wait_ge(s("constants"), 5)
            pe.wait_ge(s("query_weights"), 3)
            queries(0, 0)
            queries(0, 1)
            for b in range(-1, B + 3):
                for h in range(NH0):
                    if 0 <= b < B:
                        if h == 0:
                            pe.wait_ge(s("left_with_max"), 2 * b + 1)
                        if h == 4:
                            pe.wait_ge(s("left_with_max"), 2 * b + 2)
                        if b == 0 and h == 1:
                            pe.wait_ge(s("gates"), 1)
                        scores_kq(b, h)
                    if b + 1 < B:
                        if h in (0, 4):
                            pe.wait_ge(s("left"), 2 * (b + 1) + 1 + h // 4)
                            pe.wait_ge(s("right"), 2 * (b + 1) + 1 + h // 4)
                        scores_qk(b + 1, h)
                    if h == 0 and b + 2 < B:
                        queries(b + 2, 0)
                    if h == 2 and b + 2 < B:
                        queries(b + 2, 1)
                    if h == 7 and b + 1 < B:
                        values(b + 1)
                    if h == 3 and 2 <= b <= B + 1:
                        project(b - 2)
                    if h in (4, 5, 6, 7) and 1 <= b <= B:
                        weigh(b - 1, (h - 4) // 2, (h - 4) % 2)
                    if b == -1:
                        modulation(h)
                        if h == 1:
                            gate_rows()
                    if h == 1 and 0 <= b < B:
                        max_rows(b, 1)
                    if (b, h) in EARLY:
                        what = EARLY[b, h]
                        if what < 2:
                            pe.wait_ge(s("left"), 2 * B - 1 + what)
                            pe.wait_ge(s("right_parts"), 2 * B - 1 + what)
                        if what < CH:
                            pe.wait_ge(s("ln_high1"), what + 1)
                            pe.wait_ge(s("ln_low1"), what + 1)
                        if what < CH:
                            project_v(pe, 0, what)
                        else:
                            project_qk(pe, what - CH)
                    if h == 3 and b >= 3:
                        if b < B:
                            pe.wait_ge(s("left_with_max"), 2 * (b + 1))
                        else:
                            pe.wait_ge(s("ln_modulated1"), b - 3)
                        ln_transposes(pe, "1", b - 3, bank_m)
                    if h == 5 and b + 1 < B:
                        max_rows(b + 1, 0)

        @blk.scalar
        def _(act):
            act.wait_ge(s_ld["cond"], 16)
            for lo, hi in MASK_PARTS:
                act.activation(c_hi[:, lo:hi, :], rbc[0:2, lo:hi, :], ACT.Copy).then_inc(s("mask_high"), 1)
            act.wait_ge(s_ld["small0"], 16)

            def stack(b, n, what):
                two = slice(2 * n, 2 * n + 2)
                if what == 0:
                    act.wait_ge(s("queries"), 2 * b + n + 1)
                    if b >= 1:
                        act.wait_ge(s("left"), 2 * b - 1 + n)
                    act.activation(zh[:, two, :].rearrange("p g t -> p (g t)"), bank_z[n][:, :], ACT.Copy)\
                       .then_inc(s("queries_high"), 1)
                elif what == 1:
                    if b >= 1:
                        act.wait_ge(s("right"), 2 * b - 1 + n)
                    act.activation(zr[:, two, :].rearrange("p g t -> p (g t)"), bank_z[n][:, :], ACT.Identity,
                                   bias=role[:, 3:4], scale=role[:, 2:3])
                else:
                    act.activation(zrh[:, two, :].rearrange("p g t -> p (g t)"), bank_z[n][:, :], ACT.Identity,
                                   bias=role[:, 6:7], scale=role[:, 5:6]).then_inc(s("right_parts"), 1)

            def value_cols(b):
                act.wait_ge(s("values"), b + 1)
                if b == 0:
                    act.wait_ge(s("value_columns_zeroed"), 2)
                if b >= 2:
                    act.wait_ge(s("weighed"), 4 * (b - 1))
                v = bank_m[:, 0:2 * P].rearrange("p (k a je) -> p k a je", k=2, a=2)
                for a in range(2):
                    for k in range(2):
                        last = act.activation(vp[b % 2][:, k, 4 * a:4 * a + 4, 16 * a:16 * a + 16],
                                              v[:, k, a, :].rearrange("p (j e) -> p j e", e=DK), ACT.Copy)
                last.then_inc(s("value_columns"), 1)

            for n in range(2):
                for what in range(3):
                    stack(0, n, what)
            stack_slots = {1: (0, 0), 2: (0, 1), 3: (0, 2), 5: (1, 0), 6: (1, 1), 7: (1, 2)}
            for b in range(-1, B + 3):
                for h in range(NH0):
                    if 0 <= b < B:
                        n = b * NH0 + h
                        act.wait_ge(s("scores_k"), n + 1)
                        if n >= RING:
                            act.wait_ge(s("weighed"), 2 * ((n - RING) // 4 + 1))
                        act.activation(pt[:, n % RING, :, :].rearrange("p k t -> p (k t)"), bank_s[n % 2][:, :], ACT.Exp)\
                           .then_inc(s("exps"), 1)
                    if h == 0 and 0 <= b < B:
                        value_cols(b)
                    if h in stack_slots and b + 2 < B:
                        stack(b + 2, *stack_slots[h])
                    if (b, h) in EARLY:
                        what = EARLY[b, h]
                        if what < CH:
                            evacuate_v(act, 0, what)
                        else:
                            evacuate_qk(act, what - CH)
                    if h == 4 and b >= 3:
                        ln_modulate(act, "1", b - 3, bank_m, 0)

        @blk.vector
        def _(dve):
            dve.wait_ge(s_ld["small0"], 16)
            for i, (lo, hi) in enumerate(MASK_PARTS):
                dve.wait_ge(s("mask_high"), i + 1)
                a = lo // CH
                dve.scalar_tensor_tensor(out=r_rows[a][:, lo - a * CH:hi - a * CH, :],
                                         in0=c_hi[:, lo:hi, :].bitcast(F32), scalar=role[0:2, 4:5],
                                         in1=rbc[0:2, lo:hi, :], op0=ALU.mult, op1=ALU.add)\
                   .then_inc(s("mask_rows"), 1)

            def left_op(b, n):
                dve.wait_ge(s("right_parts"), 2 * b + n + 1)
                if b >= 2:
                    dve.wait_ge(s("scores_q"), (b - 1) * NH0)
                    dve.wait_ge(s("left_with_max"), 2 * (b - 1))
                two = slice(2 * n, 2 * n + 2)
                dve.scalar_tensor_tensor(
                    out=left[b % 2][:, two, :].rearrange("p g t -> p (g t)"),
                    in0=zh[:, two, :].rearrange("p g t -> p (g t)").bitcast(F32), scalar=role[:, 0:1],
                    in1=bank_z[n][:, :], op0=ALU.mult, op1=ALU.add).then_inc(s("left"), 1)

            def max_split(b, half):
                n = 2 * b + half
                dve.wait_ge(s("row_max"), b * NH0 + 4 * half + 4)
                src = nmax[:, 4 * half:4 * half + 4, :]
                hi = nmax_h[:, 4 * half:4 * half + 4, :]
                dve.tensor_copy(hi, src).then_inc(s("max_high"), 1)
                dve.wait_ge(s("max_high"), n + 1)
                if n == 0:
                    dve.wait_ge(s("max_columns_zeroed"), 1)
                if n >= 2:
                    dve.wait_ge(s("max_rows"), n - 1)
                dst = mx[:, half, :, :, :].rearrange("p k g (i r) -> p g i k r", i=2)
                s4 = src.rearrange("p (g i) k -> p g i k", i=2)
                h4 = hi.rearrange("p (g i) k -> p g i k", i=2).bitcast(F32)
                dve.tensor_copy(dst[:, :, :, :, MAX_ROW], h4)
                dve.tensor_tensor(dst[:, :, :, :, MAX_ROW + 1], s4, h4, ALU.subtract).then_inc(s("max_columns"), 1)

            def left_with_max(b, half):
                n = 2 * b + half
                dve.wait_ge(s("max_rows"), n + 1)
                if b >= 1:
                    dve.wait_ge(s("scores_k"), (b - 1) * NH0 + 4 * (half + 1))
                dve.wait_ge(s("left"), 2 * b + 1 + half)
                dve.tensor_tensor(leftm[:, 2 * half:2 * half + 2, :].rearrange("p g t -> p (g t)"),
                                  bank_m[:, :],
                                  left[b % 2][:, 2 * half:2 * half + 2, :].rearrange("p g t -> p (g t)").bitcast(F32),
                                  ALU.add).then_inc(s("left_with_max"), 1)

            def modulation_rows():
                dve.wait_ge(s("shift_scale_products"), 8)
                for l in range(2):
                    last = dve.tensor_tensor(mod[:, 4 * l:4 * l + 4, :],
                                             bank_c[:, 4 * B * l:4 * B * (l + 1)].rearrange("p (i b) -> p i b", b=B),
                                             ada_bt[:, 6 * l:6 * l + 4].unsqueeze(2).to_broadcast([P, 4, B]), ALU.add)
                last.then_inc(s("modulation_biased"), 1)
                dve.tensor_scalar(q_bias[:, :], qkv_bt[:, 0:NH1], SCALE1, None, ALU.mult)
                dve.wait_ge(s("modulation_biased"), 1)
                scales = mod[:, :, :].rearrange("p (l i) b -> p l i b", l=2)[:, :, 2:4, :]
                dve.tensor_scalar(scales, scales, 1.0, None, ALU.add).then_inc(s("modulation"), 1)

            def gates_biased():
                dve.wait_ge(s("gate_products"), 1)
                dve.tensor_tensor(gates[:, :, :], bank_s[1][0:B, :].rearrange("p (g n) -> p g n", g=2),
                                  gate_b[:, :, :], ALU.add).then_inc(s("gates"), 1)

            def inverse_sums(b, i):
                if i == 0:
                    dve.wait_ge(s("weighed"), 4 * b + 4)
                w = T // 2
                dve.reciprocal(dinv[:, i * w:(i + 1) * w], bank_c[:, T + i * w:T + (i + 1) * w]).then_inc(s("inverse_sums"), 1)

            def normalise(b):
                dve.wait_ge(s("inverse_sums"), 2 * b + 2)
                if b >= 1:
                    dve.wait_ge(s("projected"), b)
                dve.tensor_tensor(cn[:, :], bank_c[:, 0:T], dinv[:, :], ALU.mult).then_inc(s("normalised"), 1)

            for n in range(2):
                left_op(0, n)
            for b in range(-1, B + 3):
                for h in range(NH0):
                    if b + 1 < B:
                        n = (b + 1) * NH0 + h
                        dve.wait_ge(s("scores_q"), n + 1)
                        if h % 4 == 0 and n >= 8:
                            dve.wait_ge(s("max_columns"), 2 * b + h // 4 + 1)
                        dve.tensor_reduce(nmax[:, h, :], bank_a[n % 2][:, :].rearrange("p (k t) -> p k t", k=2),
                                          AX.X, ALU.max, negate=True).then_inc(s("row_max"), 1)
                    if h == 3 and b == -1:
                        gates_biased()
                    if h == 5 and b == 0:
                        modulation_rows()
                    if h == 1 and 0 <= b and b + 1 < B:
                        left_op(b + 1, 1)
                    if h in (0, 1) and 2 <= b <= B + 1:
                        inverse_sums(b - 2, h)
                    if h == 1 and 2 <= b <= B + 1:
                        normalise(b - 2)
                    if h == 2 and 0 <= b < B:
                        left_with_max(b, 1)
                    if h == 3 and 2 <= b <= B + 1:
                        dve.wait_ge(s("projected"), b - 1)
                        dve.tensor_tensor(xm[:, b - 2, :], bank_c[:, 0:T], xm[:, b - 2, :], ALU.add)\
                           .then_inc(s("layer0_out"), 1)
                    if h == 3 and b + 1 < B:
                        max_split(b + 1, 0)
                    if h == 4 and 2 <= b <= B + 1:
                        dve.wait_ge(s("layer0_out"), b - 1)
                        ln_stats(dve, "1", b - 2, xm)
                    if h == 5 and b + 2 < B:
                        left_op(b + 2, 0)
                    if h == 5 and 2 <= b <= B + 1:
                        ln_normal(dve, "1", b - 2, xm)
                    if h == 6 and b + 1 < B:
                        left_with_max(b + 1, 0)
                    if h == 7 and b + 1 < B:
                        max_split(b + 1, 1)

        l0.close()

        ow_raw = [sb(f"ow_raw{i}", [P, HPG, DIM]) for i in range(2)]
        ow_h = sb("ow_h", [P, NH1, DIM], F32R)
        ow_l = sb("ow_l", [P, NH1, DIM], F32R)
        prob = sb("prob", [P, 2, CH, D])
        prob_t = sb("prob_t", [P, 2, CH, D])
        at_h = sb("at_h", [P, 2, HPG, CT], F32R)
        at_l = sb("at_l", [P, 2, HPG, CT], F32R)
        nm1 = sb("nm1", [P, 2, CH])
        warm = sb("warm", [P, 1])
        sum1 = sb("sum1", [P, 2, CH])
        rs1 = sb("rs1", [P, 2, CH])

        ctx2 = ExitStack()
        blk = ctx2.enter_context(nc.Block())
        bank_s1 = banks[2:4]
        bank_t1, bank_v1, bank_o1, bank_g = banks[4], banks[5], banks[6], banks[7]
        w1_h = w_qk_h[:, :, :, :].rearrange("p k s n -> p k (s n)")
        w1_l = w_qk_l[:, :, :, :].rearrange("p k s n -> p k (s n)")
        w2_h = w_v_h[:, :, :, :].rearrange("p a k n -> p (a k n)").rearrange("p (m n) -> p m n", m=MB)
        w2_l = w_v_l[:, :, :, :].rearrange("p a k n -> p (a k n)").rearrange("p (m n) -> p m n", m=MB)

        h_h = at_h[:, :, :, :].rearrange("p a j n -> p (a j) n")
        h_l = at_l[:, :, :, :].rearrange("p a j n -> p (a j) n")
        h_f = v_sb[:, :, :, :].rearrange("p a j n -> p (a j) n")

        @blk.sync
        def _(sp):
            def load_ow(g):
                if g >= 2:
                    sp.wait_ge(s("out_weights_split"), g - 1)
                sp.dma_start(ow_raw[g % 2][:, :, :],
                             out_w.rearrange("(h p) n -> p h n", p=P)[:, g * HPG:(g + 1) * HPG, :])\
                  .then_inc(s(f"ld_ow{g % 2}"), 16)

            load_ow(0)
            load_ow(1)
            for g in range(2, GROUPS):
                load_ow(g)
                sp.wait_ge(s("weights_split"), 5 * (g - 1))
                load_group(sp, g)
            sp.wait_ge(s("weights_split"), 5 * (GROUPS - 1))
            sp.dma_start(w1_raw, ffn_w1.rearrange("(k p) n -> p k n", p=P)).then_inc(s("ld_w1"), 16)
            sp.wait_ge(s("weights_split"), 5 * GROUPS)
            sp.dma_start(w2_raw, ffn_w2.rearrange("(m p) n -> p m n", p=P)).then_inc(s("ld_w2"), 16)
            for b in range(B):
                sp.wait_ge(s("final"), b + 1)
                sp.dma_start(out[b], xm[:, b, :]).then_inc(s("stored"), 16)
            sp.wait_ge(s("stored"), 16 * B)

        MBH = MB // 2
        last_banks = [bank_o1, bank_s1[0], bank_s1[1], bank_v1]

        mb_order = [a * HPG + j for j in range(HPG) for a in range(2)]

        @blk.gpsimd
        def _(pool):
            for g in range(GROUPS):
                hs = slice(g * HPG, (g + 1) * HPG)
                raw = ow_raw[g % 2][:, :, :]
                pool.wait_ge(s(f"ld_ow{g % 2}"), 16 * (g // 2 + 1))
                pool.tensor_copy(ow_h[:, hs, :], raw).then_inc(s("out_weights_high"), 1)
                pool.wait_ge(s("out_weights_high"), g + 1)
                pool.tensor_tensor(ow_l[:, hs, :], raw, ow_h[:, hs, :].bitcast(F32), ALU.subtract)\
                    .then_inc(s("out_weights_split"), 1)
                if g + 1 < GROUPS:
                    split_v(pool, g + 1)
                    for j in range(HPG):
                        split_qk(pool, g + 1, j)
            pool.wait_ge(s("ld_w2"), 16)
            pool.wait_ge(s("projections"), proj_no[("v", HGROUPS - 3, CH - 1)] + 1)
            pool.tensor_copy(w2_h[:, 0:MBH, :], w2_raw[:, 0:MBH, :]).then_inc(s("w2h_even"), 1)
            pool.wait_ge(s("w2h_even"), 1)
            pool.tensor_tensor(w2_l[:, 0:MBH, :], w2_raw[:, 0:MBH, :], w2_h[:, 0:MBH, :].bitcast(F32),
                               ALU.subtract).then_inc(s("w2_even"), 1)
            pool.wait_ge(s("ld_w1"), 16)
            def base(b):
                pool.tensor_tensor(xm[:, b, :], xm[:, b, :], acc[:, b, :], ALU.add).then_inc(s("base"), 1)

            for j in range(HPG):
                split_qk(pool, GROUPS, j)
                for b in ((0,), (1, 2), (3,), ())[j]:
                    ln_rstd(pool, "2", b)
                    base(b)
            for b in range(CH, B):
                ln_rstd(pool, "2", b)
                base(b)

        @blk.tensor
        def _(pe):
            def scores(n):
                pe.wait_ge(s("projections_read"), proj_no[("k", n)] + 1)
                if n >= 2:
                    pe.wait_ge(s("exps1"), n - 1)
                for b in range(CH):
                    mm = pe.matmul(bank_s1[n % 2][:, b * D:(b + 1) * D], qk[:, n % 2, 0, b * D:(b + 1) * D],
                                   qk[:, n % 2, 1, b * D:(b + 1) * D], start=True, stop=True)
                mm.then_inc(s("scores"), 1)

            def turn_probs(n):
                pe.wait_ge(s("probs"), n + 1)
                if n >= 1:
                    pe.wait_ge(s("probs_t"), n)
                for b in range(CH):
                    mm = pe.transpose(bank_t1[:, b * D:(b + 1) * D], prob[:, n % 2, b, :], ident[:, :])
                mm.then_inc(s("probs_turned"), 1)

            def attend(n):
                m, j, g, c = part(n)
                pe.wait_ge(s("probs_t"), n + 1)
                pe.wait_ge(s("projections_read"), proj_no[("v", m, CH - 1)] + 1)
                if n >= 1:
                    pe.wait_ge(s("attention_low"), n)
                for b in range(CH):
                    mm = pe.matmul(bank_v1[:, b * D:(b + 1) * D], v_sb[:, m % 2, b, j * DH:(j + 1) * DH],
                                   prob_t[:, n % 2, b, :], start=True, stop=True)
                mm.then_inc(s("attention"), 1)

            def out_project(m, k, bank=bank_o1):
                g, c = divmod(m, 2)
                i = m * CH + k
                pe.wait_ge(s("attention_low"), HPG * (m + 1))
                pe.wait_ge(s("attention_high"), HPG * (m + 1))
                pe.wait_ge(s("out_weights_split"), g + 1)
                if 1 <= i <= CH * (HGROUPS - 1):
                    pe.wait_ge(s("accumulated"), i)
                cols = slice(k * D, (k + 1) * D)
                for j in range(HPG):
                    mm = three(pe, bank[:, 0:DIM], at_h[:, c, j, cols], at_l[:, c, j, cols],
                               ow_h[:, g * HPG + j, :], ow_l[:, g * HPG + j, :], j == 0, j == HPG - 1)
                mm.then_inc(s("out_products"), 1)

            def spread_gate(i, which, b):
                if i >= 1:
                    pe.wait_ge(s("gated"), i)
                if i == CH:
                    pe.wait_ge(s("ln_modulated2"), 2)
                pe.matmul(bank_g[:, 0:DIM], sel[:, b, :], gates[:, which, :], start=True, stop=True)\
                    .then_inc(s("gate_spread"), 1)

            for n in range(STEPS):
                m, k, g, c = part(n)
                scores(n)
                if n >= 1:
                    attend(n - 1)
                if 1 < n + 1 < STEPS:
                    project_qk(pe, n + 1)
                if m == HGROUPS - 1 and k in (1, 2):
                    spread_gate(2 * k - 1, 0, 2 * k - 1)
                    out_project(m - 1, 2 * k - 1)
                if n > 0:
                    turn_probs(n)
                if m + 1 < HGROUPS:
                    project_v(pe, m + 1, k)
                if n == 0:
                    turn_probs(n)
                if 1 <= m < HGROUPS - 1:
                    out_project(m - 1, k)
                if m == HGROUPS - 1 and k < 2:
                    spread_gate(2 * k, 0, 2 * k)
                    out_project(m - 1, 2 * k)
                if m == HGROUPS - 1 and k >= 2:
                    if k == 2:
                        pe.wait_ge(s("gated"), CH)
                    else:
                        pe.wait_ge(s("ln_modulated2"), k - 2)
                    ln_transposes(pe, "2", k - 2, bank_g)
            attend(STEPS - 1)
            pe.wait_ge(s("probs_t"), STEPS)
            ln_transposes(pe, "2", CH - 2, bank_t1)
            for k in range(CH):
                if k == 0:
                    pe.wait_ge(s("accumulated"), CH * (HGROUPS - 1))
                if k == 1:
                    pe.wait_ge(s("exps1"), STEPS)
                if k == CH - 1:
                    pe.wait_ge(s("attention_low"), STEPS)
                out_project(HGROUPS - 1, k, last_banks[k])
                if k == 0:
                    pe.wait_ge(s("ln_modulated2"), CH - 1)
                    ln_transposes(pe, "2", CH - 1, bank_t1)

            for c in range(2):
                for q, mb in enumerate(mb_order):
                    i = c * MB + q
                    if c == 0:
                        pe.wait_ge(s("weights_split"), 5 * GROUPS + 1 + q // 2)
                    if q == 0:
                        pe.wait_ge(s("ln_high2"), CH * (c + 1))
                        pe.wait_ge(s("ln_low2"), CH * (c + 1))
                    if c == 0 and q % 2 == 0:
                        spread_gate(CH + q // 2, 0, CH + q // 2)
                    if i < 2:
                        pe.wait_ge(s("projections_read"), len(order))
                    else:
                        pe.wait_ge(s("hidden"), i - 1)
                    for t in range(KT):
                        cols = slice(mb * P, (mb + 1) * P)
                        mm = three(pe, bank_p[i % 2][:, :], w1_h[:, t, cols], w1_l[:, t, cols],
                                   xh[:, t, c * CT:(c + 1) * CT], xl[:, t, c * CT:(c + 1) * CT],
                                   t == 0, t == KT - 1)
                    mm.then_inc(s("hidden_products"), 1)
                for k in range(CH):
                    b = c * CH + k
                    if b == 0:
                        pe.wait_ge(s("w2_even"), 1)
                        pe.wait_ge(s("w2_odd"), 1)
                        pe.wait_ge(s("accumulated"), CH * HGROUPS)
                    if b >= 2:
                        pe.wait_ge(s("ffn_biased"), b - 1)
                    for q, mb in enumerate(mb_order):
                        pe.wait_ge(s("hidden_low"), MB * c + q + 1)
                        cols = slice(k * D, (k + 1) * D)
                        mm = three(pe, bank_s1[b % 2][:, 0:DIM], h_h[:, q, cols], h_l[:, q, cols],
                                   w2_h[:, mb, :], w2_l[:, mb, :], q == 0, q == MB - 1)
                        if q == MBH:
                            spread_gate(B + b, 1, b)
                        if q == MBH and c == 0:
                            pe.wait_ge(s("ln_modulated2"), CH + k)
                            ln_transposes(pe, "2", CH + k, bank_t1)
                    mm.then_inc(s("ffn_products"), 1)

        @blk.scalar
        def _(act):
            def attention_high(n):
                m, j, g, c = part(n)
                h = g * HPG + j
                act.wait_ge(s("attention"), n + 1)
                if m >= 2:
                    act.wait_ge(s("out_products"), CH * (m - 1))
                act.activation(at_h[:, c, j, :], bank_v1[:, :], ACT.Identity,
                               bias=qkv_bt[:, 2 * NH1 + h:2 * NH1 + h + 1], scale=1.0).then_inc(s("attention_high"), 1)

            for n in range(STEPS):
                m, k, g, c = part(n)
                act.wait_ge(s("row_max1"), n + 1)
                if n >= 2:
                    act.wait_ge(s("probs_turned"), n - 1)
                    act.wait_ge(s("inverse_sums1"), n - 1)
                for b in range(CH):
                    last = act.activation(prob[:, n % 2, b, :], bank_s1[n % 2][:, b * D:(b + 1) * D], ACT.Exp,
                                          bias=nm1[:, n % 2, b:b + 1], scale=1.0,
                                          accum_out=sum1[:, n % 2, b:b + 1])
                last.then_inc(s("exps1"), 1)
                if n >= 1:
                    attention_high(n - 1)
                if n == STEPS - 1:
                    act.activation(warm[:, :], nm1[:, n % 2, 0:1], ACT.Gelu)
                if 1 < n + 1 < STEPS:
                    evacuate_qk(act, n + 1)
                if m + 1 < HGROUPS:
                    evacuate_v(act, m + 1, k)
                if m == HGROUPS - 1 and k >= 2:
                    ln_modulate(act, "2", k - 2, bank_g, 4)
                if n == STEPS - 4:
                    act.wait_ge(s("ld_w2"), 16)
                    act.wait_ge(s("projections"), proj_no[("v", HGROUPS - 1, CH - 1)] + 1)
                    act.activation(w2_h[:, MBH:, :], w2_raw[:, MBH:, :], ACT.Copy).then_inc(s("w2h_odd"), 1)
            attention_high(STEPS - 1)
            ln_modulate(act, "2", CH - 2, bank_t1, 4)
            ln_modulate(act, "2", CH - 1, bank_t1, 4)
            for c in range(2):
                for q, mb in enumerate(mb_order):
                    i = c * MB + q
                    act.wait_ge(s("hidden_products"), i + 1)
                    if c == 0:
                        act.wait_ge(s("attention"), STEPS - HPG if q < MBH else STEPS)
                        act.wait_ge(s("out_products"), CH * (HGROUPS - 1) if q < MBH else CH * HGROUPS)
                    else:
                        act.wait_ge(s("hidden_low"), q + 1)
                    act.activation(h_f[:, q, :], bank_p[i % 2][:, :], ACT.Gelu, bias=b1_t[:, mb:mb + 1], scale=1.0)\
                       .then_inc(s("hidden"), 1)
                    act.wait_ge(s("hidden"), i + 1)
                    if c == 1:
                        act.wait_ge(s("ffn_products"), CH)
                    act.activation(h_h[:, q, :], h_f[:, q, :], ACT.Copy).then_inc(s("hidden_high"), 1)
                for k in range(CH if c == 0 else 0):
                    ln_modulate(act, "2", CH + k, bank_t1, 4)

        @blk.vector
        def _(dve):
            def attention_low(n):
                m, j, g, c = part(n)
                h = g * HPG + j
                dve.wait_ge(s("attention_high"), n + 1)
                dve.scalar_tensor_tensor(out=at_l[:, c, j, :], in0=bank_v1[:, :],
                                         scalar=qkv_bt[:, 2 * NH1 + h:2 * NH1 + h + 1],
                                         in1=at_h[:, c, j, :].bitcast(F32), op0=ALU.add, op1=ALU.subtract)\
                   .then_inc(s("attention_low"), 1)

            def accumulate(m, k, bank=bank_o1):
                g, c = divmod(m, 2)
                b = c * CH + k
                dve.wait_ge(s("out_products"), m * CH + k + 1)
                if g >= 1:
                    dve.wait_ge(s("accumulated"), (m - 2) * CH + k + 1)
                dve.tensor_tensor(acc[:, b, :], bank[:, 0:DIM], out_b_bc[:, :] if g == 0 else acc[:, b, :],
                                  ALU.add).then_inc(s("accumulated"), 1)

            def add_gated(b):
                dve.wait_ge(s("gate_spread"), b + 1)
                dve.wait_ge(s("accumulated"), (HGROUPS - 2) * CH + b + 1)
                dve.tensor_tensor(acc[:, b, :], acc[:, b, :], bank_g[:, 0:DIM], ALU.mult).then_inc(s("gated"), 1)

            def residual(b):
                dve.wait_ge(s("gated"), b + 1)
                dve.tensor_tensor(acc[:, b, :], acc[:, b, :], xm[:, b, :], ALU.add).then_inc(s("residual"), 1)
                dve.wait_ge(s("residual"), b + 1)
                ln_stats(dve, "2", b, acc)

            for n in range(STEPS):
                m, k, g, c = part(n)
                dve.wait_ge(s("scores"), n + 1)
                dve.tensor_reduce(nm1[:, n % 2, :], bank_s1[n % 2][:, :].rearrange("p (b t) -> p b t", b=CH),
                                  AX.X, ALU.max, negate=True).then_inc(s("row_max1"), 1)
                if m == HGROUPS - 1:
                    for b in ((), (0,), (1, 2), (3,))[k]:
                        residual(b)
                if n == STEPS - 3:
                    dve.wait_ge(s("w2h_odd"), 1)
                    dve.tensor_tensor(w2_l[:, MBH:, :], w2_raw[:, MBH:, :], w2_h[:, MBH:, :].bitcast(F32),
                                      ALU.subtract).then_inc(s("w2_odd"), 1)
                if n == STEPS - 1:
                    ln_low(dve, "2", 0)
                dve.wait_ge(s("exps1"), n + 1)
                dve.reciprocal(rs1[:, n % 2, :], sum1[:, n % 2, :]).then_inc(s("inverse_sums1"), 1)
                dve.wait_ge(s("inverse_sums1"), n + 1)
                dve.tensor_tensor(prob[:, n % 2, :, :], prob[:, n % 2, :, :],
                                  rs1[:, n % 2, :].unsqueeze(2).to_broadcast([P, CH, D]), ALU.mult)\
                   .then_inc(s("probs"), 1)
                if m == HGROUPS - 1 and k >= 2:
                    ln_normal(dve, "2", k - 2, acc)
                if n >= 1:
                    attention_low(n - 1)
                if HPG < n <= STEPS - HPG:
                    accumulate(*divmod(n - 1 - HPG, HPG))
                if m == HGROUPS - 1 and k in (1, 2):
                    accumulate(m - 1, 2 * k - 1)
                    add_gated(2 * k - 1)
                dve.wait_ge(s("probs_turned"), n + 1)
                if n >= 2:
                    dve.wait_ge(s("attention"), n - 1)
                dve.tensor_copy(prob_t[:, n % 2, :, :].rearrange("p b t -> p (b t)"), bank_t1[:, :])\
                   .then_inc(s("probs_t"), 1)
                if m == HGROUPS - 1 and k < 2:
                    accumulate(m - 1, 2 * k)
                    add_gated(2 * k)
            ln_normal(dve, "2", 2, acc)
            attention_low(STEPS - 1)
            ln_low(dve, "2", 1)
            ln_normal(dve, "2", 3, acc)
            ln_low(dve, "2", 2)
            for k in range(CH):
                accumulate(HGROUPS - 1, k, last_banks[k])
                if k == 1:
                    ln_low(dve, "2", CH - 1)
            for c in range(2):
                for q in range(MB):
                    i = c * MB + q
                    if c == 0 and q % 2 == 0:
                        add_gated(CH + q // 2)
                    dve.wait_ge(s("hidden_high"), i + 1)
                    dve.tensor_tensor(h_l[:, q, :], h_f[:, q, :], h_h[:, q, :].bitcast(F32), ALU.subtract)\
                       .then_inc(s("hidden_low"), 1)
                    if c == 0 and q % 2 == 0:
                        residual(CH + q // 2)
                    if c == 0 and q in (MB - 4, MB - 2):
                        ln_normal(dve, "2", CH + (q - MB + 4) // 2, acc)
                for k in range(CH):
                    b = c * CH + k
                    if c == 0:
                        ln_low(dve, "2", CH + k)
                        if k + 2 < CH:
                            ln_normal(dve, "2", CH + k + 2, acc)
                    dve.wait_ge(s("ffn_products"), b + 1)
                    dve.wait_ge(s("base"), b + 1)
                    dve.tensor_tensor(acc[:, b, :], bank_s1[b % 2][:, 0:DIM], b2_bc[:, :], ALU.add).then_inc(s("ffn_biased"), 1)
                    dve.wait_ge(s("ffn_biased"), b + 1)
                    dve.wait_ge(s("gate_spread"), B + b + 1)
                    dve.tensor_tensor(acc[:, b, :], acc[:, b, :], bank_g[:, 0:DIM], ALU.mult)\
                       .then_inc(s("gated"), 1)
                    dve.wait_ge(s("gated"), B + b + 1)
                    dve.tensor_tensor(xm[:, b, :], xm[:, b, :], acc[:, b, :], ALU.add).then_inc(s("final"), 1)

        ctx2.close()


_INPUTS = ["x", "cond", "cond_t", "wq_t", "wo_t", "ada_w", "ada_b", "ada_b_t", "qkv_w", "qkv_b_t", "out_w", "out_b",
           "ffn_w1", "ffn_b1_t", "ffn_w2", "ffn_b2", "roles"]


def lay_out(inputs):
    import numpy as np
    c = np.ascontiguousarray
    i = {k: np.asarray(v) for k, v in inputs.items()}
    return {
        "x": i["x"], "cond": i["cond_2048"], "cond_t": c(i["cond_2048"].T),
        "wq_t": c(i["L0_cond_Wq"].T), "wo_t": c(i["L0_cond_Wo"].T),
        "ada_w": i["L1_cond_ada_w"], "ada_b": i["L1_cond_ada_b"],
        "ada_b_t": c(i["L1_cond_ada_b"].reshape(12, P).T),
        "qkv_w": i["L1_cond_qkv_w"], "qkv_b_t": c(i["L1_cond_qkv_b"].reshape(3 * NH1, DH).T),
        "out_w": i["L1_cond_out_w"], "out_b": i["L1_cond_out_b"],
        "ffn_w1": i["L1_cond_ffn_w1"], "ffn_b1_t": c(i["L1_cond_ffn_b1"].reshape(MB, P).T),
        "ffn_w2": i["L1_cond_ffn_w2"], "ffn_b2": i["L1_cond_ffn_b2"], "roles": row_roles(),
    }


def kernel(**inputs):
    import numpy as np
    import concourse.bacc as bacc
    from concourse.bass_utils import run_bass_kernel_spmd

    nc = bacc.Bacc("TRN2", target_bir_lowering=False, num_devices=1)
    arrays = lay_out(inputs)
    aps = {n: nc.dram_tensor(n + "_dram", a.shape, mybir.dt.from_np(a.dtype), kind="ExternalInput").ap()
           for n, a in arrays.items()}
    aps["out"] = nc.dram_tensor("out_dram", (B, D, DIM), F32, kind="ExternalOutput").ap()
    build_program(nc, **aps)
    result = run_bass_kernel_spmd(nc, [{n + "_dram": a for n, a in arrays.items()}], core_ids=[0])
    return result.results[0]["out_dram"]
```
